# Optimizing a Trainium2 kernel written in Bass

```python
import numpy as np
import jax
import jax.numpy as jnp

def _softmax(x, axis=-1):
    return jax.nn.softmax(x, axis=axis)
def _gelu(x):
    return jax.nn.gelu(x, approximate=True)
def _silu(x):
    return jax.nn.silu(x)
def _sigmoid(x):
    return jax.nn.sigmoid(x)
def _layernorm(x, axis=-1, eps=1e-5):
    m = jnp.mean(x, axis=axis, keepdims=True)
    v = jnp.var(x, axis=axis, keepdims=True)
    return (x - m) / jnp.sqrt(v + eps)
def _scatter_add(tgt, idx, src, axis=0):
    return tgt.at[idx].add(src)
def _segment_sum(src, seg, n):
    return jax.ops.segment_sum(src, seg, n)

kernel_name = 'mk_conv_seq_d4_conv_nchw16_77a9bd'

def setup_inputs(seed: int = 0):
    np.random.seed(seed)
    _w = jnp.asarray
    def _rec_inputs():
        import jax
        import jax.numpy as jnp
        _gk = jax.random.key(seed)
        x = -0.0003929 + 0.9999 * jax.random.normal(jax.random.fold_in(_gk, 1), (4, 16, 512, 512), jnp.float32)
        return x
    x = _rec_inputs()
    def _L0_conv_setup():
        import jax, jax.numpy as jnp
        import numpy as np
        C = 16
        HEADS = 2
        WS = 8
        HID = 64

        def _aff(x, alpha, beta, color):
            return x @ color.T * alpha + beta
        key = jax.random.key(seed)
        ks = jax.random.split(key, 8)
        B, H, W = (4, 512, 512)
        n = lambda k, s: jax.random.normal(k, s, jnp.float32) * 0.02
        return {'x': jax.random.normal(ks[0], (B, C, H, W), jnp.float32), 'pos_w': n(ks[1], (C, 1, 3, 3)), 'pos_b': jnp.zeros((C,), jnp.float32), 'alpha1': jnp.ones((1, 1, C), jnp.float32), 'beta1': jnp.zeros((1, 1, C), jnp.float32), 'color1': jnp.eye(C, dtype=jnp.float32), 'qkv_w': n(ks[2], (3 * C, C)), 'qkv_b': jnp.zeros((3 * C,), jnp.float32), 'proj_w': n(ks[3], (C, C)), 'proj_b': jnp.zeros((C,), jnp.float32), 'alpha2': jnp.ones((1, 1, C), jnp.float32), 'beta2': jnp.zeros((1, 1, C), jnp.float32), 'color2': jnp.eye(C, dtype=jnp.float32), 'fc1_w': n(ks[4], (HID, C)), 'fc1_b': jnp.zeros((HID,), jnp.float32), 'fc2_w': n(ks[5], (C, HID)), 'fc2_b': jnp.zeros((C,), jnp.float32)}
    _L0_conv_all = _L0_conv_setup()
    _L0_conv_in = {k: v for k, v in _L0_conv_all.items() if k in ('pos_w', 'pos_b', 'alpha1', 'beta1', 'color1', 'qkv_w', 'qkv_b', 'proj_w', 'proj_b', 'alpha2', 'beta2', 'color2', 'fc1_w', 'fc1_b', 'fc2_w', 'fc2_b', )}
    del _L0_conv_all

    def _L1_conv_setup():
        import jax, jax.numpy as jnp
        import numpy as np

        def _conv2d_same(x, w, b):
            y = jax.lax.conv_general_dilated(x, w, window_strides=(1, 1), padding=((1, 1), (1, 1)), dimension_numbers=('NCHW', 'OIHW', 'NCHW'))
            return y + b[None, :, None, None]
        key = jax.random.key(seed)
        ks = jax.random.split(key, 5)
        B, C, H, W = (16, 16, 512, 512)
        K = 3
        bound = float(np.sqrt(1.0 / (C * K * K)))
        x = jax.random.normal(ks[0], (B, C, H, W), dtype=jnp.float32)
        w1 = jax.random.uniform(ks[1], (C, C, K, K), minval=-bound, maxval=bound, dtype=jnp.float32)
        b1 = jax.random.uniform(ks[2], (C,), minval=-bound, maxval=bound, dtype=jnp.float32)
        w2 = jax.random.uniform(ks[3], (C, C, K, K), minval=-bound, maxval=bound, dtype=jnp.float32)
        b2 = jax.random.uniform(ks[4], (C,), minval=-bound, maxval=bound, dtype=jnp.float32)
        return {'x': x, 'w1': w1, 'b1': b1, 'w2': w2, 'b2': b2}
    _L1_conv_all = _L1_conv_setup()
    _L1_conv_in = {k: v for k, v in _L1_conv_all.items() if k in ('w1', 'b1', 'w2', 'b2', )}
    del _L1_conv_all

    def _L2_conv_setup():
        import jax, jax.numpy as jnp
        import numpy as np

        def _conv2d_same(x, w, b):
            y = jax.lax.conv_general_dilated(x, w, window_strides=(1, 1), padding=((1, 1), (1, 1)), dimension_numbers=('NCHW', 'OIHW', 'NCHW'))
            return y + b[None, :, None, None]
        key = jax.random.key(seed)
        ks = jax.random.split(key, 5)
        B, C, H, W = (16, 16, 512, 512)
        K = 3
        bound = float(np.sqrt(1.0 / (C * K * K)))
        x = jax.random.normal(ks[0], (B, C, H, W), dtype=jnp.float32)
        w1 = jax.random.uniform(ks[1], (C, C, K, K), minval=-bound, maxval=bound, dtype=jnp.float32)
        b1 = jax.random.uniform(ks[2], (C,), minval=-bound, maxval=bound, dtype=jnp.float32)
        w2 = jax.random.uniform(ks[3], (C, C, K, K), minval=-bound, maxval=bound, dtype=jnp.float32)
        b2 = jax.random.uniform(ks[4], (C,), minval=-bound, maxval=bound, dtype=jnp.float32)
        return {'x': x, 'w1': w1, 'b1': b1, 'w2': w2, 'b2': b2}
    _L2_conv_all = _L2_conv_setup()
    _L2_conv_in = {k: v for k, v in _L2_conv_all.items() if k in ('w1', 'b1', 'w2', 'b2', )}
    del _L2_conv_all

    def _L3_conv_setup():
        import jax, jax.numpy as jnp
        import numpy as np

        def _conv2d_same(x, w, b):
            y = jax.lax.conv_general_dilated(x, w, window_strides=(1, 1), padding=((1, 1), (1, 1)), dimension_numbers=('NCHW', 'OIHW', 'NCHW'))
            return y + b[None, :, None, None]
        key = jax.random.key(seed)
        ks = jax.random.split(key, 5)
        B, C, H, W = (16, 16, 512, 512)
        K = 3
        bound = float(np.sqrt(1.0 / (C * K * K)))
        x = jax.random.normal(ks[0], (B, C, H, W), dtype=jnp.float32)
        w1 = jax.random.uniform(ks[1], (C, C, K, K), minval=-bound, maxval=bound, dtype=jnp.float32)
        b1 = jax.random.uniform(ks[2], (C,), minval=-bound, maxval=bound, dtype=jnp.float32)
        w2 = jax.random.uniform(ks[3], (C, C, K, K), minval=-bound, maxval=bound, dtype=jnp.float32)
        b2 = jax.random.uniform(ks[4], (C,), minval=-bound, maxval=bound, dtype=jnp.float32)
        return {'x': x, 'w1': w1, 'b1': b1, 'w2': w2, 'b2': b2}
    _L3_conv_all = _L3_conv_setup()
    _L3_conv_in = {k: v for k, v in _L3_conv_all.items() if k in ('w1', 'b1', 'w2', 'b2', )}
    del _L3_conv_all

    return {
        "x": x,
        "L0_conv_pos_w": _L0_conv_in["pos_w"],
        "L0_conv_pos_b": _L0_conv_in["pos_b"],
        "L0_conv_alpha1": _L0_conv_in["alpha1"],
        "L0_conv_beta1": _L0_conv_in["beta1"],
        "L0_conv_color1": _L0_conv_in["color1"],
        "L0_conv_qkv_w": _L0_conv_in["qkv_w"],
        "L0_conv_qkv_b": _L0_conv_in["qkv_b"],
        "L0_conv_proj_w": _L0_conv_in["proj_w"],
        "L0_conv_proj_b": _L0_conv_in["proj_b"],
        "L0_conv_alpha2": _L0_conv_in["alpha2"],
        "L0_conv_beta2": _L0_conv_in["beta2"],
        "L0_conv_color2": _L0_conv_in["color2"],
        "L0_conv_fc1_w": _L0_conv_in["fc1_w"],
        "L0_conv_fc1_b": _L0_conv_in["fc1_b"],
        "L0_conv_fc2_w": _L0_conv_in["fc2_w"],
        "L0_conv_fc2_b": _L0_conv_in["fc2_b"],
        "L1_conv_w1": _L1_conv_in["w1"],
        "L1_conv_b1": _L1_conv_in["b1"],
        "L1_conv_w2": _L1_conv_in["w2"],
        "L1_conv_b2": _L1_conv_in["b2"],
        "L2_conv_w1": _L2_conv_in["w1"],
        "L2_conv_b1": _L2_conv_in["b1"],
        "L2_conv_w2": _L2_conv_in["w2"],
        "L2_conv_b2": _L2_conv_in["b2"],
        "L3_conv_w1": _L3_conv_in["w1"],
        "L3_conv_b1": _L3_conv_in["b1"],
        "L3_conv_w2": _L3_conv_in["w2"],
        "L3_conv_b2": _L3_conv_in["b2"],
    }

def reference(x, L0_conv_pos_w, L0_conv_pos_b, L0_conv_alpha1, L0_conv_beta1, L0_conv_color1, L0_conv_qkv_w, L0_conv_qkv_b, L0_conv_proj_w, L0_conv_proj_b, L0_conv_alpha2, L0_conv_beta2, L0_conv_color2, L0_conv_fc1_w, L0_conv_fc1_b, L0_conv_fc2_w, L0_conv_fc2_b, L1_conv_w1, L1_conv_b1, L1_conv_w2, L1_conv_b2, L2_conv_w1, L2_conv_b1, L2_conv_w2, L2_conv_b2, L3_conv_w1, L3_conv_b1, L3_conv_w2, L3_conv_b2):
    import jax
    import jax.numpy as jnp
    def _L0_conv_ref(x, pos_w, pos_b, alpha1, beta1, color1, qkv_w, qkv_b, proj_w, proj_b, alpha2, beta2, color2, fc1_w, fc1_b, fc2_w, fc2_b):
        import jax, jax.numpy as jnp
        import numpy as np
        C = 16
        HEADS = 2
        WS = 8
        HID = 64

        def _aff(x, alpha, beta, color):
            return x @ color.T * alpha + beta
        B, Cc, H, W = x.shape
        pos = jax.lax.conv_general_dilated(x, pos_w, window_strides=(1, 1), padding=((1, 1), (1, 1)), dimension_numbers=('NCHW', 'OIHW', 'NCHW'), feature_group_count=Cc)
        x = x + pos + pos_b[None, :, None, None]
        xt = jnp.transpose(x.reshape(B, Cc, H * W), (0, 2, 1))
        shortcut = xt
        y = _aff(xt, alpha1, beta1, color1).reshape(B, H, W, Cc)
        nH, nW = (H // WS, W // WS)
        win = y.reshape(B, nH, WS, nW, WS, Cc).transpose(0, 1, 3, 2, 4, 5)
        win = win.reshape(B * nH * nW, WS * WS, Cc)
        B_, N, _ = win.shape
        hd = Cc // HEADS
        qkv = (win @ qkv_w.T + qkv_b).reshape(B_, N, 3, HEADS, hd)
        qkv = qkv.transpose(2, 0, 3, 1, 4)
        q, k, v = (qkv[0] * hd ** (-0.5), qkv[1], qkv[2])
        attn = jax.nn.softmax(jnp.einsum('bhnd,bhmd->bhnm', q, k), axis=-1)
        out = jnp.einsum('bhnm,bhmd->bhnd', attn, v)
        out = out.transpose(0, 2, 1, 3).reshape(B_, N, Cc)
        out = out @ proj_w.T + proj_b
        out = out.reshape(B, nH, nW, WS, WS, Cc).transpose(0, 1, 3, 2, 4, 5)
        out = out.reshape(B, H * W, Cc)
        x = shortcut + out
        h1 = jax.nn.gelu(_aff(x, alpha2, beta2, color2) @ fc1_w.T + fc1_b, approximate=False)
        x = x + (h1 @ fc2_w.T + fc2_b)
        return jnp.transpose(x, (0, 2, 1)).reshape(B, Cc, H, W)

    def _L1_conv_ref(x, w1, b1, w2, b2):
        import jax, jax.numpy as jnp
        import numpy as np

        def _conv2d_same(x, w, b):
            y = jax.lax.conv_general_dilated(x, w, window_strides=(1, 1), padding=((1, 1), (1, 1)), dimension_numbers=('NCHW', 'OIHW', 'NCHW'))
            return y + b[None, :, None, None]
        out = _conv2d_same(x, w1, b1)
        out = jax.nn.relu(out)
        out = _conv2d_same(out, w2, b2)
        return out + x

    def _L2_conv_ref(x, w1, b1, w2, b2):
        import jax, jax.numpy as jnp
        import numpy as np

        def _conv2d_same(x, w, b):
            y = jax.lax.conv_general_dilated(x, w, window_strides=(1, 1), padding=((1, 1), (1, 1)), dimension_numbers=('NCHW', 'OIHW', 'NCHW'))
            return y + b[None, :, None, None]
        out = _conv2d_same(x, w1, b1)
        out = jax.nn.relu(out)
        out = _conv2d_same(out, w2, b2)
        return out + x

    def _L3_conv_ref(x, w1, b1, w2, b2):
        import jax, jax.numpy as jnp
        import numpy as np

        def _conv2d_same(x, w, b):
            y = jax.lax.conv_general_dilated(x, w, window_strides=(1, 1), padding=((1, 1), (1, 1)), dimension_numbers=('NCHW', 'OIHW', 'NCHW'))
            return y + b[None, :, None, None]
        out = _conv2d_same(x, w1, b1)
        out = jax.nn.relu(out)
        out = _conv2d_same(out, w2, b2)
        return out + x

    def _gn(v, G=8, eps=1e-5):
        B_, C_, H_, W_ = v.shape
        g = v.reshape(B_, G, C_ // G, H_, W_)
        m = jnp.mean(g, axis=(2, 3, 4), keepdims=True)
        s = jnp.var(g, axis=(2, 3, 4), keepdims=True)
        return ((g - m) / jnp.sqrt(s + eps)).reshape(v.shape)

    def _ln_c(v, eps=1e-6):
        m = jnp.mean(v, axis=1, keepdims=True)
        s = jnp.var(v, axis=1, keepdims=True)
        return (v - m) / jnp.sqrt(s + eps)

    def _ln_t(v, eps=1e-5):
        m = jnp.mean(v, axis=-1, keepdims=True)
        s = jnp.var(v, axis=-1, keepdims=True)
        return (v - m) / jnp.sqrt(s + eps)

    def _to_tokens(v):
        B_, C_, H_, W_ = v.shape
        return v.reshape(B_, C_, H_ * W_).transpose(0, 2, 1)
    def _from_tokens(t, like):
        B_, C_, H_, W_ = like.shape
        return t.transpose(0, 2, 1).reshape(B_, C_, H_, W_)

    x = _L0_conv_ref(x, L0_conv_pos_w, L0_conv_pos_b, L0_conv_alpha1, L0_conv_beta1, L0_conv_color1, L0_conv_qkv_w, L0_conv_qkv_b, L0_conv_proj_w, L0_conv_proj_b, L0_conv_alpha2, L0_conv_beta2, L0_conv_color2, L0_conv_fc1_w, L0_conv_fc1_b, L0_conv_fc2_w, L0_conv_fc2_b)
    x = _L1_conv_ref(x, L1_conv_w1, L1_conv_b1, L1_conv_w2, L1_conv_b2)
    x = _L2_conv_ref(x, L2_conv_w1, L2_conv_b1, L2_conv_w2, L2_conv_b2)
    x = _L3_conv_ref(x, L3_conv_w1, L3_conv_b1, L3_conv_w2, L3_conv_b2)
    return x


_drawn_inputs = setup_inputs


def setup_inputs(seed=0):
    import zlib

    import numpy as np

    out = dict(_drawn_inputs(seed))
    spreads = {'L0_conv_pos_b': (0.0, 0.1),
     'L0_conv_alpha1': (1.0, 0.6),
     'L0_conv_beta1': (0.0, 0.8),
     'L0_conv_qkv_b': (0.0, 0.8),
     'L0_conv_proj_b': (0.0, 0.1),
     'L0_conv_alpha2': (1.0, 0.6),
     'L0_conv_beta2': (0.0, 2.0),
     'L0_conv_fc1_b': (0.0, 2.0),
     'L0_conv_fc2_b': (0.0, 0.8)}
    factors = {'L0_conv_color1': 8.0,
     'L0_conv_qkv_w': 8.0,
     'L0_conv_proj_w': 7.694,
     'L0_conv_color2': 8.0,
     'L0_conv_fc1_w': 8.0,
     'L0_conv_fc2_w': 5.453,
     'L1_conv_b1': 28.512,
     'L2_conv_b1': 30.296,
     'L3_conv_b1': 31.224,
     'L1_conv_b2': 26.431,
     'L2_conv_b2': 27.129,
     'L3_conv_b2': 27.628}
    for name, (base, spread) in spreads.items():
        noise = np.random.default_rng([zlib.crc32(name.encode()), seed]).standard_normal(out[name].shape)
        drawn = base * np.exp(spread * noise) if base else spread * noise
        out[name] = jnp.asarray(drawn.astype(out[name].dtype))
    for name, factor in factors.items():
        out[name] = (out[name] * factor).astype(out[name].dtype)
    return out
```

```python
from contextlib import ExitStack

import concourse.bass as bass
from concourse import mybir

F32 = mybir.dt.float32
ACT = mybir.ActivationFunctionType
ALU = mybir.AluOpType
AX = mybir.AxisListType

P = 128
C = 16
R = 8
TAPS = 3
IMAGES, H, W = 4, 512, 512
BPI = H // R
NB = 4
GROUPS = IMAGES * BPI // NB
GPI = BPI // NB
PB = IMAGES * (BPI + 1) + 1
WP = W + 2
EDGE = TAPS * 2 * C
UNROLL = 4
LAG = 2


def padded(g):
    return g * NB + g // GPI


def load_edges(q, tile, above, below, g, done):
    for tap in range(TAPS):
        for t, src, skip in ((0, above, 0), (1, below, 2)):
            p0 = (tap * 2 + t) * C
            q.dma_start(tile[p0:p0 + C, :, TAPS - 1 - tap:TAPS - 1 - tap + W],
                        src[:, bass.ds(padded(g) + skip, NB), :]).then_inc(done, 16)


EDGE_LOADS = 2 * TAPS


def convolve(nc, out, taps, x, edge, first_wait=None):
    for tap in range(TAPS):
        for n in range(NB):
            nc.tensor.matmul(out[n][:, :], taps[:, tap, :], x[:, n, tap:tap + W], start=(tap == 0), stop=False)
    if first_wait:
        first_wait()
    for n in range(NB):
        last = nc.tensor.matmul(out[n][:, :], taps[0:EDGE, TAPS, :], edge[:, n, 1:1 + W], start=False, stop=True)
    return last


def within(t, first, end):
    return not isinstance(t, int) or first <= t < end


def steps(eng, body, last_step):
    for t in range(UNROLL):
        body(t, t, t // 2)
    rounds = GROUPS // UNROLL
    with eng.Fori(1, rounds) as k:
        for u in range(UNROLL):
            body(k * UNROLL + u, u, k * (UNROLL // 2) + u // 2)
    for t in range(GROUPS, last_step + 1):
        body(t, t % UNROLL, t // 2)


def zero_borders(nc, padded_tensors, edge_tensors):
    with ExitStack() as ctx:
        zeros = ctx.enter_context(nc.sbuf_tensor("zeros", [P, IMAGES + 1, W], F32))
        zeroed = ctx.enter_context(nc.semaphore("zeroed"))
        stored = ctx.enter_context(nc.semaphore("borders_stored"))
        block = ctx.enter_context(nc.Block())

        @block.vector
        def _(dve):
            nc.vector.memset(zeros[:, :, :], 0.0).then_inc(zeroed, 1)

        @block.sync
        def _(sp):
            sp.wait_ge(zeroed, 1)
            n = 0
            for t in padded_tensors:
                sp.dma_start(t.rearrange("b p x -> p b x")[:, ::BPI + 1, :], zeros[:, :, :]).then_inc(stored, 16)
                n += 1
            for e in edge_tensors:
                for which in range(2):
                    sp.dma_start(e[which].rearrange("b c x -> c b x")[:, ::BPI + 1, :],
                                 zeros[0:C, :, :]).then_inc(stored, 16)
                    n += 1
            sp.wait_ge(stored, 16 * n)


def position_conv(nc, x, taps_d, center_d, bias_d, edges, y):
    with ExitStack() as ctx:
        sb = lambda name, shape: ctx.enter_context(nc.sbuf_tensor(name, shape, F32))
        sem = lambda name: ctx.enter_context(nc.semaphore(name))
        taps = sb("pos_taps", [P, TAPS + 1, P])
        center = sb("pos_center", [P, P])
        bias = sb("pos_bias", [P, 1])
        xt = [sb(f"pos_x{s}", [P, NB, WP]) for s in range(UNROLL)]
        et = [sb(f"pos_edge{s}", [EDGE, NB, WP]) for s in range(UNROLL)]
        yt = [sb(f"pos_y{s}", [P, NB, W]) for s in range(2)]
        ps = [[ctx.enter_context(nc.psum_tensor(f"pos_ps{s}_{n}", [P, W], F32)) for n in range(NB)] for s in range(2)]
        weights_in, weights_ready, cleared, edges_made = sem("p_win"), sem("p_wready"), sem("p_clear"), sem("p_edges")
        x_in = [sem(f"p_x_in{s}") for s in range(UNROLL)]
        e_in = [sem(f"p_e_in{s}") for s in range(UNROLL)]
        conv_done, y_ready = sem("p_conv"), sem("p_y")
        y_out = [sem(f"p_y_out{s}") for s in range(2)]
        block = ctx.enter_context(nc.Block())

        @block.sync
        def _(sp):
            sp.dma_start(taps[:, :, :], taps_d).then_inc(weights_in, 16)
            sp.dma_start(center[:, :], center_d).then_inc(weights_in, 16)
            sp.dma_start(bias[:, :], bias_d).then_inc(weights_in, 16)
            for which, row in ((0, 0), (1, R - 1)):
                for b in range(IMAGES):
                    at = b * (BPI + 1) + 1
                    sp.dma_start(edges[which, at:at + BPI].rearrange("i c w -> i c w"),
                                 x[b].rearrange("c (i r) w -> r i c w", r=R)[row]).then_inc(edges_made, 16)
            sp.wait_ge(cleared, 2 * UNROLL)

            def load(t, s, half):
                if isinstance(t, int) and t >= GROUPS:
                    return
                if not isinstance(t, int) or t >= UNROLL:
                    sp.wait_ge(conv_done, t - UNROLL + 1)
                for r in range(R):
                    src = x.rearrange("b c h w -> c b (h w)")
                    off = (t % GPI) * (NB * R * W)
                    win = src[:, t // GPI, bass.ds(off, NB * R * W)]
                    win = win.rearrange("c (n r w) -> r c n w", r=R, w=W)[r]
                    sp.dma_start(xt[s][r * C:(r + 1) * C, :, 1:1 + W], win).then_inc(x_in[s], 16)
                if isinstance(t, int) and t == 0:
                    sp.wait_ge(edges_made, 16 * 2 * IMAGES)
                load_edges(sp, et[s], edges[1].rearrange("b c w -> c b w"),
                           edges[0].rearrange("b c w -> c b w"), t, e_in[s])
            steps(sp, load, GROUPS - 1)

        @block.gpsimd
        def _(pool):
            for s in range(UNROLL):
                nc.gpsimd.memset(xt[s][:, :, :], 0.0).then_inc(cleared, 1)
            for s in range(UNROLL):
                nc.gpsimd.memset(et[s][:, :, :], 0.0).then_inc(cleared, 1)
            def store(t, s, half):
                pool.wait_ge(y_ready, (t + 1))
                for r in range(R):
                    dst = y.rearrange("b (c r) w -> r c b w", r=R)[r][:, bass.ds(padded(t) + 1, NB), :]
                    pool.dma_start(dst, yt[s % 2][r * C:(r + 1) * C, :, :]).then_inc(y_out[s % 2], 16)
            steps(pool, store, GROUPS - 1)
            for s in range(2):
                pool.wait_ge(y_out[s], 16 * R * GROUPS // 2)

        @block.vector
        def _(dve):
            dve.wait_ge(weights_in, 48)
            nc.vector.tensor_tensor(taps[:, 1, :], taps[:, 1, :], center[:, :], ALU.add).then_inc(weights_ready, 1)

        @block.tensor
        def _(pe):
            pe.wait_ge(weights_ready, 1)
            def conv(t, s, half):
                pe.wait_ge(x_in[s], (t // UNROLL + 1) * 16 * R)
                if not isinstance(t, int) or t >= 2:
                    pe.wait_ge(y_ready, t - 1)
                def edge_wait():
                    pe.wait_ge(e_in[s], (t // UNROLL + 1) * 16 * EDGE_LOADS)
                convolve(nc, ps[s % 2], taps, xt[s], et[s], edge_wait).then_inc(conv_done, 1)
            steps(pe, conv, GROUPS - 1)

        @block.scalar
        def _(act):
            act.wait_ge(weights_in, 48)
            def evacuate(t, s, half):
                act.wait_ge(conv_done, t + 1)
                if not isinstance(t, int) or t >= 2:
                    act.wait_ge(y_out[s % 2], half * 16 * R)
                for n in range(NB):
                    last = nc.scalar.activation(yt[s % 2][:, n, :], ps[s % 2][n][:, :], ACT.Identity, bias=bias[:, 0:1])
                last.then_inc(y_ready, 1)
            steps(act, evacuate, GROUPS - 1)


def residual_pair(nc, name, taps1_d, taps2_d, b1_d, b2_d, src, src_rows_inner, dst, dst_image, h_edges):
    with ExitStack() as ctx:
        sb = lambda what, shape: ctx.enter_context(nc.sbuf_tensor(f"{name}_{what}", shape, F32))
        sem = lambda what: ctx.enter_context(nc.semaphore(f"{name}_{what}"))
        taps1, taps2 = sb("taps1", [P, TAPS + 1, P]), sb("taps2", [P, TAPS + 1, P])
        b1, b2 = sb("b1", [P, 1]), sb("b2", [P, 1])
        xt = [sb(f"x{s}", [P, NB, WP]) for s in range(UNROLL)]
        ht = [sb(f"h{s}", [P, NB, WP]) for s in range(UNROLL)]
        xe = [sb(f"x_edge{s}", [EDGE, NB, WP]) for s in range(UNROLL)]
        he = [sb(f"h_edge{s}", [EDGE, NB, WP]) for s in range(2)]
        yt = [sb(f"y{s}", [P, NB, W]) for s in range(2)]
        ps1 = [ctx.enter_context(nc.psum_tensor(f"{name}_ps1_{n}", [P, W], F32)) for n in range(NB)]
        ps2 = [ctx.enter_context(nc.psum_tensor(f"{name}_ps2_{n}", [P, W], F32)) for n in range(NB)]
        weights_in, cleared = sem("weights_in"), sem("cleared")
        x_in, xe_in = [sem(f"x_in{s}") for s in range(UNROLL)], [sem(f"xe_in{s}") for s in range(UNROLL)]
        he_in = [sem(f"he_in{s}") for s in range(2)]
        conv1_done, h_ready, h_edges_out = sem("conv1_done"), sem("h_ready"), sem("h_edges_out")
        conv2_done, y_ready = sem("conv2_done"), sem("y_ready")
        y_out = [sem(f"y_out{s}") for s in range(2)]
        x_loads = R if src_rows_inner else 1
        y_stores = R if dst_image else 1
        block = ctx.enter_context(nc.Block())

        @block.sync
        def _(sp):
            for tile, d in ((taps1[:, :, :], taps1_d), (taps2[:, :, :], taps2_d), (b1[:, :], b1_d), (b2[:, :], b2_d)):
                sp.dma_start(tile, d).then_inc(weights_in, 16)
            sp.wait_ge(cleared, 4 * UNROLL)
            if src_rows_inner:
                above, below = (src.rearrange("b (c r) w -> r c b w", r=R)[r] for r in (R - 1, 0))
            else:
                above, below = (src.rearrange("b (r c) w -> r c b w", r=R)[r] for r in (R - 1, 0))

            def load(t, s, half):
                if within(t, UNROLL, GROUPS):
                    sp.wait_ge(y_ready, t - UNROLL + 1)
                blocks = bass.ds(padded(t) + 1, NB)
                if src_rows_inner:
                    for r in range(R):
                        sp.dma_start(xt[s][r * C:(r + 1) * C, :, 1:1 + W],
                                     src.rearrange("b (c r) w -> r c b w", r=R)[r][:, blocks, :]).then_inc(x_in[s], 16)
                else:
                    sp.dma_start(xt[s][:, :, 1:1 + W], src[blocks].rearrange("b p w -> p b w")).then_inc(x_in[s], 16)
                load_edges(sp, xe[s], above, below, t, xe_in[s])
            steps(sp, load, GROUPS - 1)

        @block.gpsimd
        def _(pool):
            for tile in xt + xe + ht:
                nc.gpsimd.memset(tile[:, :, :], 0.0).then_inc(cleared, 1)
            for tile in he + yt:
                nc.gpsimd.memset(tile[:, :, :], 0.0).then_inc(cleared, 1)
            pool.wait_ge(cleared, 4 * UNROLL)

            def move(t, s, half):
                if within(t, 0, GROUPS):
                    pool.wait_ge(h_ready, t + 1)
                    for which, p0 in ((0, 0), (1, P - C)):
                        pool.dma_start(h_edges[which].rearrange("b c w -> c b w")[:, bass.ds(padded(t) + 1, NB), :],
                                       ht[s][p0:p0 + C, :, 1:1 + W]).then_inc(h_edges_out, 16)
                if within(t, 1, GROUPS + 1):
                    g, gs = t - 1, (s - 1) % 2
                    pool.wait_ge(h_edges_out, 32 * min(t + 1, GROUPS) if isinstance(t, int) else 32 * (t + 1))
                    if within(t, 3, GROUPS + 1):
                        pool.wait_ge(conv2_done, t - 2)
                    load_edges(pool, he[gs], h_edges[1].rearrange("b c w -> c b w"),
                               h_edges[0].rearrange("b c w -> c b w"), g, he_in[gs])
                if within(t, 3, GROUPS + 3):
                    g, gs = t - 3, (s - 3) % 2
                    pool.wait_ge(y_ready, t - 2)
                    if dst_image:
                        image = dst.rearrange("b c h w -> c b (h w)")[:, g // GPI, bass.ds(g % GPI * (NB * R * W), NB * R * W)]
                        image = image.rearrange("c (n r w) -> r c n w", r=R, w=W)
                        for r in range(R):
                            pool.dma_start(image[r], yt[gs][r * C:(r + 1) * C, :, :]).then_inc(y_out[gs], 16)
                    else:
                        pool.dma_start(dst[bass.ds(padded(g) + 1, NB)].rearrange("b p w -> p b w"),
                                       yt[gs][:, :, :]).then_inc(y_out[gs], 16)
            steps(pool, move, GROUPS + 2)
            for s in range(2):
                pool.wait_ge(y_out[s], 16 * y_stores * GROUPS // 2)

        @block.tensor
        def _(pe):
            pe.wait_ge(weights_in, 64)

            def conv(t, s, half):
                if within(t, 0, GROUPS):
                    pe.wait_ge(x_in[s], (t // UNROLL + 1) * 16 * x_loads)
                    if within(t, 1, GROUPS):
                        pe.wait_ge(h_ready, t)
                    convolve(nc, ps1, taps1, xt[s], xe[s],
                             lambda: pe.wait_ge(xe_in[s], (t // UNROLL + 1) * 16 * EDGE_LOADS)).then_inc(conv1_done, 1)
                if within(t, LAG, GROUPS + LAG):
                    gs = (s - LAG) % UNROLL
                    pe.wait_ge(h_ready, t - LAG + 1)
                    if within(t, LAG + 1, GROUPS + LAG):
                        pe.wait_ge(y_ready, t - LAG)
                    convolve(nc, ps2, taps2, ht[gs], he[gs % 2],
                             lambda: pe.wait_ge(he_in[gs % 2], half * 16 * EDGE_LOADS)).then_inc(conv2_done, 1)
            steps(pe, conv, GROUPS + LAG - 1)

        @block.scalar
        def _(act):
            act.wait_ge(weights_in, 64)
            act.wait_ge(cleared, 4 * UNROLL)

            def hidden(t, s, half):
                act.wait_ge(conv1_done, t + 1)
                if within(t, UNROLL, GROUPS):
                    act.wait_ge(conv2_done, t - UNROLL + 1)
                    act.wait_ge(h_edges_out, 32 * (t - UNROLL + 1))
                for n in range(NB):
                    last = nc.scalar.activation(ht[s][:, n, 1:1 + W], ps1[n][:, :], ACT.Relu, bias=b1[:, 0:1])
                last.then_inc(h_ready, 1)
            steps(act, hidden, GROUPS - 1)

        @block.vector
        def _(dve):
            dve.wait_ge(weights_in, 64)
            dve.wait_ge(cleared, 4 * UNROLL)

            def residual(t, s, half):
                if not within(t, LAG, GROUPS + LAG):
                    return
                gs = (s - LAG) % UNROLL
                dve.wait_ge(conv2_done, t - LAG + 1)
                if within(t, LAG + 2, GROUPS + LAG):
                    dve.wait_ge(y_out[gs % 2], (half - 1) * 16 * y_stores)
                for n in range(NB):
                    last = nc.vector.scalar_tensor_tensor(yt[gs % 2][:, n, :], ps2[n][:, :], b2[:, 0:1],
                                                          xt[gs][:, n, 1:1 + W], ALU.add, ALU.add)
                last.then_inc(y_ready, 1)
            steps(dve, residual, GROUPS + LAG - 1)


SB = P // C
WS = 8
TOK = WS * WS
PAIRS = SB // 2
UW = 128
WIN = UW // WS
UPS = W // UW
UNITS = IMAGES * BPI // SB * UPS
HALF = 512
HALVES = 2
HW_ = UW // HALVES
WPH = WIN // HALVES
HEADS, HD = 2, C // 2
HID = 64
VC = C + HEADS
PARTS = 3
KROWS = PARTS * 2 * C
F16 = mybir.dt.float16


def attention_mlp(nc, w_d, x, qk_dram, y):
    with ExitStack() as ctx:
        sb = lambda name, shape, dt=F32: ctx.enter_context(nc.sbuf_tensor("at_" + name, shape, dt))
        sem = lambda name: ctx.enter_context(nc.semaphore("at_" + name))
        bank = lambda name: ctx.enter_context(nc.psum_tensor("at_ps_" + name, [P, 512], F32))
        scores, scores_t, weighted, misc = ([bank(f"{n}{i}") for i in range(2)] for n in ("s", "t", "o", "m"))

        w = {name: sb(name, list(d.shape)) for name, d in w_d.items()}
        wqkv = sb("wqkv", [P, 3, P])
        bqkv = sb("bqkv", [P, 3])
        w1, b1 = sb("w1", [P, PAIRS, P]), sb("b1", [P, 1])
        bproj, by = sb("bproj", [P, 1]), sb("by", [P, 1])
        scratch = sb("scratch", [P, PAIRS, P])

        xt = [sb(f"x{s}", [P, R, UW]) for s in range(2)]
        qk_split = [sb(f"qk{s}", [P, 4, HALVES * HALF], F16) for s in range(2)]
        q_sided = sb("q_sided", [P, 2, WIN, 2, TOK], F16)
        ones = sb("ones", [P, WIN])
        x_twice = sb("x_twice", [P, WIN, HEADS, TOK])
        qs = [sb(f"qs{s}", [KROWS, PAIRS, WIN * 2 * TOK], F16) for s in range(2)]
        ks = [sb(f"ks{s}", [KROWS, HEADS, PAIRS, HALVES * HALF], F16) for s in range(2)]
        vt = [sb(f"v{s}", [P, WIN, SB, VC]) for s in range(2)]
        top = [sb(f"max{i}", [P, PAIRS * HEADS]) for i in range(2)]
        shifted = [sb(f"shifted{i}", [P, 512]) for i in range(2)]
        probs = [sb(f"probs{i}", [P, 512]) for i in range(2)]
        inv = [sb(f"inv{i}", [P, 2 * SB, HEADS]) for i in range(2)]
        att = [sb(f"att{i}", [P, 2, P]) for i in range(2)]
        att_t = [sb(f"att_t{s}", [P, WIN, P]) for s in range(2)]
        z = sb("z", [P, HALVES, HALF])
        hid = sb("hid", [P, HALVES, PAIRS, HALF])
        yt = [sb(f"y{s}", [P, R, UW]) for s in range(2)]

        with ExitStack() as c2:
            sem2 = lambda name: c2.enter_context(nc.semaphore("prep_" + name))
            loaded, scaled, product, copied, cleared = (sem2(n) for n in ("loaded", "scaled", "product", "copied", "cleared"))
            block = c2.enter_context(nc.Block())

            @block.sync
            def _(sp):
                for name, d in w_d.items():
                    sp.dma_start(w[name][tuple(slice(None) for _ in d.shape)], d).then_inc(loaded, 16)

            @block.gpsimd
            def _(pool):
                nc.gpsimd.memset(ones[:, :], 1.0).then_inc(cleared, 1)
                for t in ks:
                    nc.gpsimd.memset(t[:, :, :, :], 0.0).then_inc(cleared, 1)
                for t in vt:
                    nc.gpsimd.memset(t[:, :, :, :], 0.0).then_inc(cleared, 1)
                pool.wait_ge(cleared, 5)
                for t in vt:
                    for h in range(HEADS):
                        nc.gpsimd.memset(t[h * TOK:(h + 1) * TOK, :, :, C + h:C + h + 1], 1.0).then_inc(cleared, 1)

            @block.vector
            def _(dve):
                dve.wait_ge(loaded, 16 * len(w_d))
                cols = w["cols"]
                for i in range(3):
                    nc.vector.tensor_scalar(scratch[:, i, :], w["qkv"][:, i, :], cols[:, 0:1],
                                            HD ** -0.5 if i == 0 else 1.0, ALU.mult, ALU.mult).then_inc(scaled, 1)
                dve.wait_ge(product, 1)
                nc.vector.tensor_copy(wqkv[:, :, :], misc[0][:, 0:3 * P].rearrange("p (i c) -> p i c", i=3)).then_inc(copied, 1)
                nc.vector.tensor_tensor(bqkv[:, :], misc[1][:, 0:3], cols[:, 4:7], ALU.add).then_inc(copied, 1)
                dve.wait_ge(copied, 2)
                nc.vector.tensor_scalar(bqkv[:, 0:1], bqkv[:, 0:1], HD ** -0.5, None, ALU.mult).then_inc(copied, 1)
                for p in range(PAIRS):
                    nc.vector.tensor_scalar(scratch[:, p, :], w["fc1"][:, p, :], cols[:, 2:3], None, ALU.mult).then_inc(scaled, 1)
                dve.wait_ge(product, 2)
                nc.vector.tensor_copy(w1[:, :, :], misc[0][:, :].rearrange("p (i c) -> p i c", i=PAIRS)).then_inc(copied, 1)
                nc.vector.tensor_tensor(bproj[:, :], misc[1][:, 3:4], cols[:, 7:8], ALU.add).then_inc(copied, 1)
                dve.wait_ge(copied, 5)
                nc.vector.tensor_tensor(by[:, :], bproj[:, :], cols[:, 9:10], ALU.add).then_inc(copied, 1)
                dve.wait_ge(product, 3)
                nc.vector.tensor_tensor(b1[:, :], misc[1][:, 4:5], cols[:, 8:9], ALU.add).then_inc(copied, 1)

            @block.tensor
            def _(pe):
                pe.wait_ge(loaded, 16 * len(w_d))
                cols = w["cols"]
                for i in range(3):
                    nc.tensor.matmul(misc[1][:, i:i + 1], w["qkv"][:, i, :], cols[:, 1:2], start=True, stop=True)
                pe.wait_ge(scaled, 3)
                for i in range(3):
                    last = nc.tensor.matmul(misc[0][:, i * P:(i + 1) * P], w["color1"][:, :], scratch[:, i, :], start=True, stop=True)
                last.then_inc(product, 1)
                pe.wait_ge(copied, 3)
                pe.wait_ge(scaled, 3 + PAIRS)
                for a in range(2):
                    nc.tensor.matmul(misc[1][:, 3:4], w["proj"][:, a, :], bqkv[:, 2:3], start=(a == 0), stop=(a == 1))
                for p in range(PAIRS):
                    last = nc.tensor.matmul(misc[0][:, p * P:(p + 1) * P], w["color2"][:, :], scratch[:, p, :], start=True, stop=True)
                last.then_inc(product, 1)
                pe.wait_ge(copied, 5)
                nc.tensor.matmul(misc[1][:, 4:5], w["fc1"][:, 0, :], cols[:, 3:4], start=True, stop=False)
                nc.tensor.matmul(misc[1][:, 4:5], w1[:, 0, :], bproj[:, 0:1], start=False, stop=True).then_inc(product, 1)

        x_copied, q_sided_ready = sem("x_copied"), sem("q_sided_ready")
        x_in = [sem(f"x_in{s}") for s in range(2)]
        qk_parted, qk_out = sem("qk_parted"), sem("qk_out")
        qk_in = [sem(f"qk_in{s}") for s in range(2)]
        projected, qk_done, v_done, s_done, t_done, pv_done, att_turned = (sem(n) for n in (
            "projected", "qk_done", "v_done", "s_done", "t_done", "pv_done", "att_turned"))
        qk_high, v_ready, max_ready, shifted_ready, probs_ready, inv_ready, att_ready, att_t_ready = (sem(n) for n in (
            "qk_high", "v_ready", "max_ready", "shifted_ready", "probs_ready", "inv_ready", "att_ready", "att_t_ready"))
        z_ready, fc1_done, hid_ready, fc2_done, y_ready = (sem(n) for n in ("z_ready", "fc1_done", "hid_ready", "fc2_done", "y_ready"))
        y_out = [sem(f"y_out{s}") for s in range(2)]
        block = ctx.enter_context(nc.Block())

        QK_LOADS = PARTS * (1 + 2 * HEADS)
        QN, KN = WIN * 2 * TOK, HALVES * HALF
        LAST = UNITS + 1
        has_mlp = lambda u: within(u, 2, UNITS + 2)
        has_att = lambda u: within(u, 1, UNITS + 1)
        has_in = lambda u: within(u, 0, UNITS)

        def unit_at(sup, quarter):
            return lambda t: t[bass.ds(sup * SB + sup // (BPI // SB) + 1, SB)].rearrange(
                "b (c r) w -> (b c) r w", r=R)[:, :, bass.ds(quarter * UW, UW)]

        def run(eng, body, lag=0):
            for u in range(4):
                v = max(u - lag, 0)
                body(u, u % 2, unit_at(v // UPS, v % UPS))
            with eng.Fori(2, UNITS // 2) as k:
                m = k - lag // 2
                for s in range(2):
                    body(k * 2 + s, s, unit_at(m // 2, m % 2 * 2 + s))
            for u in range(UNITS, LAST + 1):
                v = u - lag
                body(u, u % 2, unit_at(v // UPS, v % UPS))

        @block.sync
        def _(sp):
            def move(u, s, window):
                if not has_in(u):
                    return
                if within(u, 2, UNITS):
                    sp.wait_ge(z_ready, HALVES * (u - 1))
                sp.dma_start(xt[s][:, :, :], window(x)).then_inc(x_in[s], 16)
                if within(u, 2, UNITS):
                    sp.wait_ge(s_done, WIN * (u - 1))
                sp.wait_ge(qk_parted, 4 * u + 4)
                sp.dma_start(qk_dram[s][:, 2 * QN:], qk_split[s][:, 2:4, :].rearrange("p i n -> p (i n)")).then_inc(qk_out, 16)
                sp.wait_ge(q_sided_ready, 4 * u + 4)
                sp.dma_start(qk_dram[s][:, 0:2 * QN], q_sided[:, :, :, :, :].rearrange("p i w a n -> p (i w a n)")).then_inc(qk_out, 16)
                sp.wait_ge(qk_out, 32 * (u + 1))
                sides = qk_dram[s].rearrange("(p a c) n -> a c p n", a=2, c=C)
                pair = qk_dram[s].rearrange("(p q) n -> q p n", q=2 * C)
                for part in range(PARTS):
                    iq, ik = int(part == 1), int(part == 2)
                    sp.dma_start(qs[s][part * 2 * C:(part + 1) * 2 * C, :, :], pair[:, :, iq * QN:(iq + 1) * QN]).then_inc(qk_in[s], 16)
                    for side in range(2):
                        for h in range(HEADS):
                            row = (part * 2 + side) * C + h * HD
                            sp.dma_start(ks[s][row:row + HD, h, :, :], sides[side][h * HD:(h + 1) * HD, :,
                                         2 * QN + ik * KN:2 * QN + (ik + 1) * KN]).then_inc(qk_in[s], 16)
            run(sp, move)

        @block.gpsimd
        def _(pool):
            def store(u, s, window):
                if has_in(u):
                    pool.wait_ge(x_in[s], (u // 2 + 1) * 16)
                    if within(u, 1, UNITS):
                        pool.wait_ge(v_done, 4 * u)
                    for h in range(HEADS):
                        nc.gpsimd.tensor_tensor(x_twice[:, :, h, :].rearrange("p w (r x) -> p w r x", x=WS),
                                                xt[s][:, :, :].rearrange("p r (w x) -> p w r x", x=WS),
                                                ones[:, :].unsqueeze(2).unsqueeze(3).to_broadcast([P, WIN, R, WS]),
                                                ALU.mult).then_inc(x_copied, 1)
                if has_mlp(u):
                    pool.wait_ge(y_ready, HALVES * (u - 1))
                    pool.dma_start(window(y), yt[s][:, :, :]).then_inc(y_out[s], 16)
                if has_in(u):
                    pool.wait_ge(qk_parted, 4 * u + 3)
                    if within(u, 1, UNITS):
                        pool.wait_ge(qk_out, 32 * u)
                    for part in range(2):
                        for side in range(2):
                            nc.gpsimd.tensor_tensor(q_sided[:, part, :, side, :],
                                                    qk_split[s][:, part, :].rearrange("p (w n) -> p w n", n=TOK),
                                                    w["sides"][:, side:side + 1].unsqueeze(2).to_broadcast([P, WIN, TOK]),
                                                    ALU.mult)\
                                .then_inc(q_sided_ready, 1)
            run(pool, store, lag=2)
            for s in range(2):
                pool.wait_ge(y_out[s], 16 * UNITS // 2)

        def columns(t, half):
            return t[:, :, half * HW_:(half + 1) * HW_]

        def by_window(t, half):
            return columns(t, half).rearrange("p r (w x) -> p w r x", x=WS)

        @block.tensor
        def _(pe):
            def mlp(u, s):
                c = u - 2
                for half in range(HALVES):
                    pe.wait_ge(att_t_ready, 4 * c + 3 + half)
                    for a in range(2):
                        last = nc.tensor.matmul(misc[half][:, :], w["proj"][:, a, :],
                                                att_t[s][:, half * WPH:(half + 1) * WPH, a * TOK:(a + 1) * TOK],
                                                start=(a == 0), stop=(a == 1))
                    last.then_inc(projected, 1)
                for i in range(HALVES * PAIRS):
                    half, p = divmod(i, PAIRS)
                    if i < 2:
                        pe.wait_ge(z_ready, HALVES * c + i + 1)
                    else:
                        pe.wait_ge(hid_ready, HALVES * PAIRS * c + i - 1)
                    nc.tensor.matmul(misc[i % 2][:, :], w1[:, p, :], z[:, half, :], start=True, stop=True).then_inc(fc1_done, 1)
                for half in range(HALVES):
                    pe.wait_ge(hid_ready, HALVES * PAIRS * c + HALVES * PAIRS - 1 + half)
                    for p in range(PAIRS):
                        last = nc.tensor.matmul(misc[half][:, :], w["fc2"][:, p, :], hid[:, half, p, :],
                                                start=(p == 0), stop=(p == PAIRS - 1))
                    last.then_inc(fc2_done, 1)

            def project(u, s):
                pe.wait_ge(x_in[s], (u // 2 + 1) * 16)
                for i in range(4):
                    half, which = divmod(i, 2)
                    if i >= 2:
                        pe.wait_ge(qk_parted, 4 * u + i - 1)
                    elif has_mlp(u):
                        pe.wait_ge(y_ready, HALVES * (u - 2) + i + 1)
                    elif u == 1:
                        pe.wait_ge(v_ready, 3 + i)
                    nc.tensor.matmul(misc[i % 2][:, :], wqkv[:, which, :], by_window(xt[s], half), start=True, stop=True)\
                        .then_inc(qk_done, 1)
                pe.wait_ge(x_copied, HEADS * (u + 1))
                for i in range(4):
                    if i < 2:
                        pe.wait_ge(qk_parted, 4 * u + 3 + i)
                    else:
                        pe.wait_ge(v_ready, 4 * u + i - 1)
                    for j in range(4):
                        both = x_twice[:, 4 * i + j, :, :].rearrange("p h n -> p (h n)")
                        last = nc.tensor.matmul(misc[i % 2][:, j * P:(j + 1) * P], both, wqkv[:, 2, :], start=True, stop=True)
                    last.then_inc(v_done, 1)

            def attend(u, s):
                b = u - 1
                s = 1 - s
                pe.wait_ge(qk_in[s], (b // 2 + 1) * 16 * QK_LOADS if isinstance(u, int) else
                           (8 * QK_LOADS * (b - s) + 16 * QK_LOADS))
                pe.wait_ge(v_ready, 4 * b + 4)
                for i in range(WIN + 8):
                    if i < WIN:
                        if within(u, 2, UNITS + 1) or i >= 2:
                            pe.wait_ge(shifted_ready, WIN * b + i - 1)
                        for p in range(PAIRS):
                            last = nc.tensor.matmul(scores[i % 2][:, p * P:(p + 1) * P], qs[s][:, p, i * P:(i + 1) * P],
                                                    ks[s][:, :, p, i * TOK:(i + 1) * TOK],
                                                    start=True, stop=True)
                        last.then_inc(s_done, 1)
                    if 1 <= i < WIN + 1:
                        j = i - 1
                        pe.wait_ge(shifted_ready, WIN * b + j + 1)
                        if within(u, 2, UNITS + 1) or j >= 2:
                            pe.wait_ge(probs_ready, WIN * b + j - 1)
                        for p in range(PAIRS):
                            last = nc.tensor.transpose(scores_t[j % 2][:, p * P:(p + 1) * P],
                                                       shifted[j % 2][:, p * P:(p + 1) * P], w["eye"][:, :])
                        last.then_inc(t_done, 1)
                    if 3 <= i < WIN + 3:
                        j = i - 3
                        pe.wait_ge(probs_ready, WIN * b + j + 1)
                        if j % 2 == 0 and (within(u, 2, UNITS + 1) or j >= 4):
                            pe.wait_ge(att_ready, WIN // 2 * b + j // 2 - 1)
                        for p in range(PAIRS):
                            c0 = (j % 2 * PAIRS + p) * 2 * VC
                            last = nc.tensor.matmul(weighted[j // 2 % 2][:, c0:c0 + 2 * VC], probs[j % 2][:, p * P:(p + 1) * P],
                                                    vt[s][:, j, 2 * p:2 * p + 2, :], start=True, stop=True)
                        last.then_inc(pv_done, 1)
                    if i >= 7 and i % 2 == 1:
                        j = (i - 7) // 2
                        if j < WIN // 2:
                            pe.wait_ge(att_ready, WIN // 2 * b + j + 1)
                            q = j // 2
                            if j % 2 == 0:
                                if q >= 2:
                                    pe.wait_ge(att_t_ready, 4 * b + q - 1)
                                elif has_in(u):
                                    pe.wait_ge(v_ready, 4 * u + 3 + q)
                                elif has_mlp(u):
                                    pe.wait_ge(y_ready, HALVES * (u - 2) + q + 1)
                            for n in range(2):
                                last = nc.tensor.transpose(misc[q % 2][:, (j % 2 * 2 + n) * P:(j % 2 * 2 + n + 1) * P],
                                                           att[j % 2][:, n, :], w["eye"][:, :])
                            last.then_inc(att_turned, 1)

            def step(u, s, _):
                if has_mlp(u):
                    mlp(u, s)
                if has_in(u):
                    project(u, s)
                if has_att(u):
                    attend(u, s)
            run(pe, step)

        @block.scalar
        def _(act):
            def step(u, s, _):
                if has_mlp(u):
                    for i in range(HALVES * PAIRS):
                        act.wait_ge(fc1_done, HALVES * PAIRS * (u - 2) + i + 1)
                        if within(u, 3, UNITS + 2) and i % PAIRS == 0:
                            act.wait_ge(fc2_done, HALVES * (u - 3) + i // PAIRS + 1)
                        nc.scalar.activation(hid[:, i // PAIRS, i % PAIRS, :], misc[i % 2][:, :], ACT.Gelu,
                                             bias=b1[:, 0:1]).then_inc(hid_ready, 1)
                if has_in(u):
                    for i in range(4):
                        half, which = divmod(i, 2)
                        act.wait_ge(qk_done, 4 * u + i + 1)
                        if i == 0 and within(u, 2, UNITS):
                            act.wait_ge(qk_out, 32 * (u - 1))
                        nc.scalar.activation(qk_split[s][:, 2 * which, half * HALF:(half + 1) * HALF], misc[i % 2][:, :],
                                             ACT.Identity, bias=bqkv[:, which:which + 1]).then_inc(qk_high, 1)
                if has_att(u):
                    b, s = u - 1, 1 - s
                    for i in range(WIN + 8):
                        if i < WIN:
                            act.wait_ge(t_done, WIN * b + i + 1)
                            if within(u, 2, UNITS + 1) or i >= 2:
                                act.wait_ge(pv_done, WIN * b + i - 1)
                            nc.scalar.activation(probs[i % 2][:, :], scores_t[i % 2][:, :], ACT.Exp).then_inc(probs_ready, 1)
                        if i >= 9 and i % 4 == 1:
                            q = (i - 9) // 4
                            act.wait_ge(att_turned, WIN // 2 * b + 2 * q + 2)
                            if q == 0 and within(u, 3, UNITS + 1):
                                act.wait_ge(projected, HALVES * (u - 2))
                            nc.scalar.copy(att_t[s][:, 4 * q:4 * q + 4, :], misc[q % 2][:, :].rearrange(
                                "p (w n) -> p w n", w=4)).then_inc(att_t_ready, 1)
            run(act, step)

        @block.vector
        def _(dve):
            def step(u, s, _):
                if has_mlp(u):
                    c = u - 2
                    for half in range(HALVES):
                        dve.wait_ge(projected, HALVES * c + half + 1)
                        if within(u, 3, UNITS + 2) and half == 0:
                            dve.wait_ge(y_ready, HALVES * c)
                        nc.vector.tensor_tensor(
                            z[:, half, :].rearrange("p (r w x) -> p r w x", r=R, x=WS),
                            misc[half][:, :].rearrange("p (w r x) -> p r w x", r=R, x=WS),
                            columns(xt[s], half).rearrange("p r (w x) -> p r w x", x=WS), ALU.add).then_inc(z_ready, 1)
                    if within(u, 4, UNITS + 2):
                        dve.wait_ge(y_out[s], (8 * (u - s) - 16) if not isinstance(u, int) else 16 * (u // 2 - 1))
                    for half in range(HALVES):
                        dve.wait_ge(fc2_done, HALVES * c + half + 1)
                        nc.vector.scalar_tensor_tensor(
                            columns(yt[s], half), misc[half][:, :].rearrange("p (r x) -> p r x", r=R), by[:, 0:1],
                            z[:, half, :].rearrange("p (r x) -> p r x", r=R), ALU.add, ALU.add).then_inc(y_ready, 1)
                if has_in(u):
                    for i in range(4):
                        half, which = divmod(i, 2)
                        high = qk_split[s][:, 2 * which, half * HALF:(half + 1) * HALF]
                        low = qk_split[s][:, 2 * which + 1, half * HALF:(half + 1) * HALF]
                        dve.wait_ge(qk_high, 4 * u + i + 1)
                        nc.vector.scalar_tensor_tensor(low, misc[i % 2][:, :], bqkv[:, which:which + 1], high,
                                                       ALU.add, ALU.subtract).then_inc(qk_parted, 1)
                    for i in range(4):
                        dve.wait_ge(v_done, 4 * u + i + 1)
                        if i == 0 and within(u, 2, UNITS):
                            dve.wait_ge(pv_done, WIN * (u - 1))
                        nc.vector.tensor_tensor(vt[s][:, 4 * i:4 * i + 4, :, 0:C].rearrange("p w g c -> p (w g) c"),
                                                misc[i % 2][:, :].rearrange("p (w c) -> p w c", c=C),
                                                w["head_mask"][:, :].unsqueeze(1).to_broadcast([P, 4 * SB, C]),
                                                ALU.mult).then_inc(v_ready, 1)
                if has_att(u):
                    b = u - 1
                    for i in range(WIN + 8):
                        if i < WIN:
                            dve.wait_ge(s_done, WIN * b + i + 1)
                            tile = scores[i % 2][:, :].rearrange("p (k m) -> p k m", m=TOK)
                            nc.vector.tensor_reduce(top[i % 2][:, :], tile, AX.X, ALU.max).then_inc(max_ready, 1)
                            dve.wait_ge(max_ready, WIN * b + i + 1)
                            if within(u, 2, UNITS + 1) or i >= 2:
                                dve.wait_ge(t_done, WIN * b + i - 1)
                            nc.vector.tensor_tensor(shifted[i % 2][:, :].rearrange("p (k m) -> p k m", m=TOK), tile,
                                                    top[i % 2][:, :].unsqueeze(2).to_broadcast([P, PAIRS * HEADS, TOK]),
                                                    ALU.subtract).then_inc(shifted_ready, 1)
                        if i >= 5 and i % 2 == 1:
                            j = (i - 5) // 2
                            if j < WIN // 2:
                                dve.wait_ge(pv_done, WIN * b + 2 * j + 2)
                                tile = weighted[j % 2][:, 0:2 * SB * VC].rearrange("p (g c) -> p g c", c=VC)
                                nc.vector.reciprocal(inv[j % 2][:, :, :], tile[:, :, C:VC]).then_inc(inv_ready, 1)
                                dve.wait_ge(inv_ready, WIN // 2 * b + j + 1)
                                if within(u, 2, UNITS + 1) or j >= 2:
                                    dve.wait_ge(att_turned, WIN // 2 * b + j - 1)
                                nc.vector.tensor_tensor(
                                    att[j % 2][:, :, :].rearrange("p w (g h d) -> p (w g) h d", h=HEADS, d=HD),
                                    tile[:, :, 0:C].rearrange("p g (h d) -> p g h d", h=HEADS),
                                    inv[j % 2][:, :, :].unsqueeze(3).to_broadcast([P, 2 * SB, HEADS, HD]),
                                    ALU.mult).then_inc(att_ready, 1)
            run(dve, step)


def program(nc, x, pos_taps, eye, pos_b, taps, conv_b, color1, qkv, proj, color2, fc1, fc2, cols, head_mask, sides, out):
    dram = lambda name, shape, dt=F32: nc.dram_tensor(name, shape, dt, kind="Internal").ap()
    y = [dram(f"y{i}", [PB, P, W]) for i in range(4)]
    edges_x = dram("edges_x", [2, PB, C, W])
    h_edges = [dram(f"edges_h{i}", [2, PB, C, W]) for i in range(3)]
    zero_borders(nc, y, [edges_x] + h_edges)
    position_conv(nc, x, pos_taps, eye, pos_b, edges_x, y[0])
    attention_mlp(nc, dict(color1=color1, qkv=qkv, proj=proj, color2=color2, fc1=fc1, fc2=fc2, cols=cols,
                           head_mask=head_mask, sides=sides, eye=eye), y[0], dram("qk", [2, P, 6 * HALVES * HALF], F16), y[1])
    for i in range(3):
        residual_pair(nc, f"layer{i + 1}", taps[2 * i], taps[2 * i + 1], conv_b[2 * i], conv_b[2 * i + 1],
                      y[i + 1], i == 0, out if i == 2 else y[i + 2], i == 2, h_edges[i])


_ORDER = ["x", "pos_taps", "eye", "pos_b", "taps", "conv_b", "color1", "qkv", "proj", "color2", "fc1", "fc2", "cols",
          "head_mask", "sides"]


def kernel(**inputs):
    import numpy as np
    import concourse.bacc as _bacc
    from concourse import mybir as _mybir
    from concourse.bass_utils import run_bass_kernel_spmd as _run

    def banded(w):
        t = np.zeros((P, TAPS + 1, P), np.float32)
        for r in range(R):
            cols = slice(r * C, (r + 1) * C)
            for ky in range(3):
                for kx in range(3):
                    r_in, m = r + ky - 1, w[:, :, ky, kx].T
                    if 0 <= r_in < R:
                        t[r_in * C:(r_in + 1) * C, kx, cols] = m
                    else:
                        p0 = (kx * 2 + (r_in == R)) * C
                        t[p0:p0 + C, TAPS, cols] = m
        return t

    a = {k: np.asarray(v) for k, v in inputs.items()}
    depthwise = np.zeros((C, C, 3, 3), np.float32)
    depthwise[np.arange(C), np.arange(C)] = a["L0_conv_pos_w"][:, 0]
    arrays = {"x": np.ascontiguousarray(a["x"]), "pos_taps": banded(depthwise), "eye": np.eye(P, dtype=np.float32),
              "pos_b": np.tile(a["L0_conv_pos_b"], R).reshape(P, 1),
              "taps": np.stack([banded(a[f"L{i}_conv_w{j}"]) for i in (1, 2, 3) for j in (1, 2)]),
              "conv_b": np.stack([np.tile(a[f"L{i}_conv_b{j}"], R).reshape(P, 1) for i in (1, 2, 3) for j in (1, 2)])}

    def diagonal(m, blocks=range(SB)):
        t = np.zeros((P, P), np.float32)
        for g in blocks:
            t[g * C:(g + 1) * C, g * C:(g + 1) * C] = m
        return t

    fc1, fc2 = np.zeros((P, PAIRS, P), np.float32), np.zeros((P, PAIRS, P), np.float32)
    for p in range(PAIRS):
        for side in range(2):
            g = 2 * p + side
            fc1[g * C:(g + 1) * C, p, side * HID:(side + 1) * HID] = a["L0_conv_fc1_w"].T
            fc2[side * HID:(side + 1) * HID, p, g * C:(g + 1) * C] = a["L0_conv_fc2_w"].T
    qkv_w, qkv_b = a["L0_conv_qkv_w"], a["L0_conv_qkv_b"]
    column = lambda v: np.tile(v.reshape(-1), P // v.size)
    mask = np.zeros((P, C), np.float32)
    for h in range(HEADS):
        mask[h * TOK:(h + 1) * TOK, h * HD:(h + 1) * HD] = 1.0
    arrays.update(
        color1=diagonal(a["L0_conv_color1"]), color2=diagonal(a["L0_conv_color2"]),
        qkv=np.stack([diagonal(qkv_w[i * C:(i + 1) * C].T) for i in range(3)], axis=1),
        proj=np.stack([diagonal(a["L0_conv_proj_w"].T, range(side, SB, 2)) for side in range(2)], axis=1),
        fc1=fc1, fc2=fc2, head_mask=mask,
        sides=np.repeat(np.tile(np.eye(2, dtype=np.float32), (PAIRS, 1)), C, axis=0),
        cols=np.stack([column(v) for v in (
            a["L0_conv_alpha1"], a["L0_conv_beta1"], a["L0_conv_alpha2"], a["L0_conv_beta2"],
            qkv_b[0:C], qkv_b[C:2 * C], qkv_b[2 * C:], a["L0_conv_proj_b"], a["L0_conv_fc1_b"], a["L0_conv_fc2_b"])], axis=1))
    nc = _bacc.Bacc("TRN2", target_bir_lowering=False, num_devices=1)
    args = [nc.dram_tensor("in_" + k, arrays[k].shape, _mybir.dt.from_np(arrays[k].dtype), kind="ExternalInput").ap()
            for k in _ORDER]
    args.append(nc.dram_tensor("out", (IMAGES, C, H, W), F32, kind="ExternalOutput").ap())
    program(nc, *args)
    r = _run(nc, [{"in_" + k: v for k, v in arrays.items()}], core_ids=[0])
    return r.results[0]["out"]
```

```python
from contextlib import ExitStack

import concourse.bass as bass
from concourse import mybir

F32 = mybir.dt.float32
ACT = mybir.ActivationFunctionType
ALU = mybir.AluOpType
AX = mybir.AxisListType

P = 128
C = 16
R = 8
TAPS = 3
IMAGES, H, W = 4, 512, 512
BPI = H // R
NB = 4
GROUPS = IMAGES * BPI // NB
GPI = BPI // NB
PB = IMAGES * (BPI + 1) + 1
WP = W + 2
EDGE = TAPS * 2 * C
UNROLL = 4
LAG = 2


def padded(g):
    return g * NB + g // GPI


def clear_borders(nc, tiles, cleared):
    for tile in tiles:
        for c0 in (0, W):
            nc.gpsimd.memset(tile[:, :, c0:c0 + 2], 0.0).then_inc(cleared, 1)


def load_edges(q, tile, above, below, g, done):
    for tap in range(TAPS):
        for t, src, skip in ((0, above, 0), (1, below, 2)):
            p0 = (tap * 2 + t) * C
            q.dma_start(tile[p0:p0 + C, :, TAPS - 1 - tap:TAPS - 1 - tap + W],
                        src[:, bass.ds(padded(g) + skip, NB), :]).then_inc(done, 16)


EDGE_LOADS = 2 * TAPS


def convolve(nc, out, taps, x, edge, first_wait=None):
    for tap in range(TAPS):
        for n in range(NB):
            nc.tensor.matmul(out[n][:, :], taps[:, tap, :], x[:, n, tap:tap + W], start=(tap == 0), stop=False)
    if first_wait:
        first_wait()
    for n in range(NB):
        last = nc.tensor.matmul(out[n][:, :], taps[0:EDGE, TAPS, :], edge[:, n, 1:1 + W], start=False, stop=True)
    return last


def within(t, first, end):
    return not isinstance(t, int) or first <= t < end


def steps(eng, body, last_step):
    for t in range(UNROLL):
        body(t, t, t // 2)
    rounds = GROUPS // UNROLL
    with eng.Fori(1, rounds) as k:
        for u in range(UNROLL):
            body(k * UNROLL + u, u, k * (UNROLL // 2) + u // 2)
    for t in range(GROUPS, last_step + 1):
        body(t, t % UNROLL, t // 2)


def zero_borders(nc, padded_tensors, edge_tensors):
    with ExitStack() as ctx:
        zeros = ctx.enter_context(nc.sbuf_tensor("zeros", [P, IMAGES + 1, W], F32))
        zeroed = ctx.enter_context(nc.semaphore("zeroed"))
        stored = ctx.enter_context(nc.semaphore("borders_stored"))
        block = ctx.enter_context(nc.Block())

        @block.vector
        def _(dve):
            nc.vector.memset(zeros[:, :, :], 0.0).then_inc(zeroed, 1)

        @block.sync
        def _(sp):
            sp.wait_ge(zeroed, 1)
            n = 0
            for t in padded_tensors:
                sp.dma_start(t.rearrange("b p x -> p b x")[:, ::BPI + 1, :], zeros[:, :, :]).then_inc(stored, 16)
                n += 1
            for e in edge_tensors:
                for which in range(2):
                    sp.dma_start(e[which].rearrange("b c x -> c b x")[:, ::BPI + 1, :],
                                 zeros[0:C, :, :]).then_inc(stored, 16)
                    n += 1
            sp.wait_ge(stored, 16 * n)


def position_conv(nc, x, taps_d, center_d, bias_d, edges, y):
    with ExitStack() as ctx:
        sb = lambda name, shape: ctx.enter_context(nc.sbuf_tensor(name, shape, F32))
        sem = lambda name: ctx.enter_context(nc.semaphore(name))
        taps = sb("pos_taps", [P, TAPS + 1, P])
        center = sb("pos_center", [P, P])
        bias = sb("pos_bias", [P, 1])
        xt = [sb(f"pos_x{s}", [P, NB, WP]) for s in range(UNROLL)]
        et = [sb(f"pos_edge{s}", [EDGE, NB, WP]) for s in range(UNROLL)]
        yt = [sb(f"pos_y{s}", [P, NB, W]) for s in range(2)]
        ps = [[ctx.enter_context(nc.psum_tensor(f"pos_ps{s}_{n}", [P, W], F32)) for n in range(NB)] for s in range(2)]
        weights_in, weights_ready, cleared, edges_made = sem("p_win"), sem("p_wready"), sem("p_clear"), sem("p_edges")
        x_in = [sem(f"p_x_in{s}") for s in range(UNROLL)]
        e_in = [sem(f"p_e_in{s}") for s in range(UNROLL)]
        conv_done, y_ready = sem("p_conv"), sem("p_y")
        y_out = [sem(f"p_y_out{s}") for s in range(2)]
        block = ctx.enter_context(nc.Block())

        @block.sync
        def _(sp):
            sp.dma_start(taps[:, :, :], taps_d).then_inc(weights_in, 16)
            sp.dma_start(center[:, :], center_d).then_inc(weights_in, 16)
            sp.dma_start(bias[:, :], bias_d).then_inc(weights_in, 16)
            for which, row in ((0, 0), (1, R - 1)):
                for b in range(IMAGES):
                    at = b * (BPI + 1) + 1
                    sp.dma_start(edges[which, at:at + BPI].rearrange("i c w -> i c w"),
                                 x[b].rearrange("c (i r) w -> r i c w", r=R)[row]).then_inc(edges_made, 16)
            sp.wait_ge(cleared, 2 * 2 * UNROLL)

            def load(t, s, half):
                if isinstance(t, int) and t >= GROUPS:
                    return
                if not isinstance(t, int) or t >= UNROLL:
                    sp.wait_ge(conv_done, t - UNROLL + 1)
                for r in range(R):
                    src = x.rearrange("b c h w -> c b (h w)")
                    off = (t % GPI) * (NB * R * W)
                    win = src[:, t // GPI, bass.ds(off, NB * R * W)]
                    win = win.rearrange("c (n r w) -> r c n w", r=R, w=W)[r]
                    sp.dma_start(xt[s][r * C:(r + 1) * C, :, 1:1 + W], win).then_inc(x_in[s], 16)
                if isinstance(t, int) and t == 0:
                    sp.wait_ge(edges_made, 16 * 2 * IMAGES)
                load_edges(sp, et[s], edges[1].rearrange("b c w -> c b w"),
                           edges[0].rearrange("b c w -> c b w"), t, e_in[s])
            steps(sp, load, GROUPS - 1)

        @block.gpsimd
        def _(pool):
            clear_borders(nc, xt + et, cleared)
            def store(t, s, half):
                pool.wait_ge(y_ready, (t + 1))
                for r in range(R):
                    dst = y.rearrange("b (c r) w -> r c b w", r=R)[r][:, bass.ds(padded(t) + 1, NB), :]
                    pool.dma_start(dst, yt[s % 2][r * C:(r + 1) * C, :, :]).then_inc(y_out[s % 2], 16)
            steps(pool, store, GROUPS - 1)
            for s in range(2):
                pool.wait_ge(y_out[s], 16 * R * GROUPS // 2)

        @block.vector
        def _(dve):
            dve.wait_ge(weights_in, 48)
            nc.vector.tensor_tensor(taps[:, 1, :], taps[:, 1, :], center[:, :], ALU.add).then_inc(weights_ready, 1)

        @block.tensor
        def _(pe):
            pe.wait_ge(weights_ready, 1)
            def conv(t, s, half):
                pe.wait_ge(x_in[s], (t // UNROLL + 1) * 16 * R)
                if not isinstance(t, int) or t >= 2:
                    pe.wait_ge(y_ready, t - 1)
                def edge_wait():
                    pe.wait_ge(e_in[s], (t // UNROLL + 1) * 16 * EDGE_LOADS)
                convolve(nc, ps[s % 2], taps, xt[s], et[s], edge_wait).then_inc(conv_done, 1)
            steps(pe, conv, GROUPS - 1)

        @block.scalar
        def _(act):
            act.wait_ge(weights_in, 48)
            def evacuate(t, s, half):
                act.wait_ge(conv_done, t + 1)
                if not isinstance(t, int) or t >= 2:
                    act.wait_ge(y_out[s % 2], half * 16 * R)
                for n in range(NB):
                    last = nc.scalar.activation(yt[s % 2][:, n, :], ps[s % 2][n][:, :], ACT.Identity, bias=bias[:, 0:1])
                last.then_inc(y_ready, 1)
            steps(act, evacuate, GROUPS - 1)


def residual_pair(nc, name, taps1_d, taps2_d, b1_d, b2_d, src, src_rows_inner, dst, dst_image, h_edges):
    with ExitStack() as ctx:
        sb = lambda what, shape: ctx.enter_context(nc.sbuf_tensor(f"{name}_{what}", shape, F32))
        sem = lambda what: ctx.enter_context(nc.semaphore(f"{name}_{what}"))
        taps1, taps2 = sb("taps1", [P, TAPS + 1, P]), sb("taps2", [P, TAPS + 1, P])
        b1, b2 = sb("b1", [P, 1]), sb("b2", [P, 1])
        xt = [sb(f"x{s}", [P, NB, WP]) for s in range(UNROLL)]
        ht = [sb(f"h{s}", [P, NB, WP]) for s in range(UNROLL)]
        xe = [sb(f"x_edge{s}", [EDGE, NB, WP]) for s in range(UNROLL)]
        he = [sb(f"h_edge{s}", [EDGE, NB, WP]) for s in range(2)]
        yt = [sb(f"y{s}", [P, NB, W]) for s in range(2)]
        ps1 = [ctx.enter_context(nc.psum_tensor(f"{name}_ps1_{n}", [P, W], F32)) for n in range(NB)]
        ps2 = [ctx.enter_context(nc.psum_tensor(f"{name}_ps2_{n}", [P, W], F32)) for n in range(NB)]
        weights_in, cleared = sem("weights_in"), sem("cleared")
        x_in, xe_in = [sem(f"x_in{s}") for s in range(UNROLL)], [sem(f"xe_in{s}") for s in range(UNROLL)]
        he_in = [sem(f"he_in{s}") for s in range(2)]
        conv1_done, h_ready, h_edges_out = sem("conv1_done"), sem("h_ready"), sem("h_edges_out")
        conv2_done, y_ready = sem("conv2_done"), sem("y_ready")
        y_out = [sem(f"y_out{s}") for s in range(2)]
        CLEARED = 2 * (3 * UNROLL + 2)
        x_loads = R if src_rows_inner else 1
        y_stores = R if dst_image else 1
        block = ctx.enter_context(nc.Block())

        @block.sync
        def _(sp):
            for tile, d in ((taps1[:, :, :], taps1_d), (taps2[:, :, :], taps2_d), (b1[:, :], b1_d), (b2[:, :], b2_d)):
                sp.dma_start(tile, d).then_inc(weights_in, 16)
            sp.wait_ge(cleared, CLEARED)
            if src_rows_inner:
                above, below = (src.rearrange("b (c r) w -> r c b w", r=R)[r] for r in (R - 1, 0))
            else:
                above, below = (src.rearrange("b (r c) w -> r c b w", r=R)[r] for r in (R - 1, 0))

            def load(t, s, half):
                if within(t, UNROLL, GROUPS):
                    sp.wait_ge(y_ready, t - UNROLL + 1)
                blocks = bass.ds(padded(t) + 1, NB)
                if src_rows_inner:
                    for r in range(R):
                        sp.dma_start(xt[s][r * C:(r + 1) * C, :, 1:1 + W],
                                     src.rearrange("b (c r) w -> r c b w", r=R)[r][:, blocks, :]).then_inc(x_in[s], 16)
                else:
                    sp.dma_start(xt[s][:, :, 1:1 + W], src[blocks].rearrange("b p w -> p b w")).then_inc(x_in[s], 16)
                load_edges(sp, xe[s], above, below, t, xe_in[s])
            steps(sp, load, GROUPS - 1)

        @block.gpsimd
        def _(pool):
            clear_borders(nc, xt + xe + ht + he, cleared)
            pool.wait_ge(cleared, CLEARED)

            def move(t, s, half):
                if within(t, 0, GROUPS):
                    pool.wait_ge(h_ready, t + 1)
                    for which, p0 in ((0, 0), (1, P - C)):
                        pool.dma_start(h_edges[which].rearrange("b c w -> c b w")[:, bass.ds(padded(t) + 1, NB), :],
                                       ht[s][p0:p0 + C, :, 1:1 + W]).then_inc(h_edges_out, 16)
                if within(t, 1, GROUPS + 1):
                    g, gs = t - 1, (s - 1) % 2
                    pool.wait_ge(h_edges_out, 32 * min(t + 1, GROUPS) if isinstance(t, int) else 32 * (t + 1))
                    if within(t, 3, GROUPS + 1):
                        pool.wait_ge(conv2_done, t - 2)
                    load_edges(pool, he[gs], h_edges[1].rearrange("b c w -> c b w"),
                               h_edges[0].rearrange("b c w -> c b w"), g, he_in[gs])
                if within(t, 3, GROUPS + 3):
                    g, gs = t - 3, (s - 3) % 2
                    pool.wait_ge(y_ready, t - 2)
                    if dst_image:
                        image = dst.rearrange("b c h w -> c b (h w)")[:, g // GPI, bass.ds(g % GPI * (NB * R * W), NB * R * W)]
                        image = image.rearrange("c (n r w) -> r c n w", r=R, w=W)
                        for r in range(R):
                            pool.dma_start(image[r], yt[gs][r * C:(r + 1) * C, :, :]).then_inc(y_out[gs], 16)
                    else:
                        pool.dma_start(dst[bass.ds(padded(g) + 1, NB)].rearrange("b p w -> p b w"),
                                       yt[gs][:, :, :]).then_inc(y_out[gs], 16)
            steps(pool, move, GROUPS + 2)
            for s in range(2):
                pool.wait_ge(y_out[s], 16 * y_stores * GROUPS // 2)

        @block.tensor
        def _(pe):
            pe.wait_ge(weights_in, 64)

            def conv(t, s, half):
                if within(t, 0, GROUPS):
                    pe.wait_ge(x_in[s], (t // UNROLL + 1) * 16 * x_loads)
                    if within(t, 1, GROUPS):
                        pe.wait_ge(h_ready, t)
                    convolve(nc, ps1, taps1, xt[s], xe[s],
                             lambda: pe.wait_ge(xe_in[s], (t // UNROLL + 1) * 16 * EDGE_LOADS)).then_inc(conv1_done, 1)
                if within(t, LAG, GROUPS + LAG):
                    gs = (s - LAG) % UNROLL
                    pe.wait_ge(h_ready, t - LAG + 1)
                    if within(t, LAG + 1, GROUPS + LAG):
                        pe.wait_ge(y_ready, t - LAG)
                    convolve(nc, ps2, taps2, ht[gs], he[gs % 2],
                             lambda: pe.wait_ge(he_in[gs % 2], half * 16 * EDGE_LOADS)).then_inc(conv2_done, 1)
            steps(pe, conv, GROUPS + LAG - 1)

        @block.scalar
        def _(act):
            act.wait_ge(weights_in, 64)
            act.wait_ge(cleared, CLEARED)

            def hidden(t, s, half):
                act.wait_ge(conv1_done, t + 1)
                if within(t, UNROLL, GROUPS):
                    act.wait_ge(conv2_done, t - UNROLL + 1)
                    act.wait_ge(h_edges_out, 32 * (t - UNROLL + 1))
                for n in range(NB):
                    last = nc.scalar.activation(ht[s][:, n, 1:1 + W], ps1[n][:, :], ACT.Relu, bias=b1[:, 0:1])
                last.then_inc(h_ready, 1)
            steps(act, hidden, GROUPS - 1)

        @block.vector
        def _(dve):
            dve.wait_ge(weights_in, 64)
            dve.wait_ge(cleared, CLEARED)

            def residual(t, s, half):
                if not within(t, LAG, GROUPS + LAG):
                    return
                gs = (s - LAG) % UNROLL
                dve.wait_ge(conv2_done, t - LAG + 1)
                if within(t, LAG + 2, GROUPS + LAG):
                    dve.wait_ge(y_out[gs % 2], (half - 1) * 16 * y_stores)
                for n in range(NB):
                    last = nc.vector.scalar_tensor_tensor(yt[gs % 2][:, n, :], ps2[n][:, :], b2[:, 0:1],
                                                          xt[gs][:, n, 1:1 + W], ALU.add, ALU.add)
                last.then_inc(y_ready, 1)
            steps(dve, residual, GROUPS + LAG - 1)


SB = P // C
WS = 8
TOK = WS * WS
PAIRS = SB // 2
UW = 128
WIN = UW // WS
UPS = W // UW
UNITS = IMAGES * BPI // SB * UPS
HALF = 512
HALVES = 2
HW_ = UW // HALVES
WPH = WIN // HALVES
HEADS, HD = 2, C // 2
HID = 64
VC = C + HEADS
PARTS = 3
KROWS = PARTS * 2 * C
TOPS = PAIRS * HEADS
TOP_SCALE = 1024.0
F16 = mybir.dt.float16
BF16 = mybir.dt.bfloat16


def attention_mlp(nc, w_d, x, y):
    with ExitStack() as ctx:
        sb = lambda name, shape, dt=F32: ctx.enter_context(nc.sbuf_tensor("at_" + name, shape, dt))
        sem = lambda name: ctx.enter_context(nc.semaphore("at_" + name))
        bank = lambda name: ctx.enter_context(nc.psum_tensor("at_ps_" + name, [P, 512], F32))
        scores, scores_t, weighted, misc = ([bank(f"{n}{i}") for i in range(2)] for n in ("s", "t", "o", "m"))

        w = {name: sb(name, list(d.shape)) for name, d in w_d.items()}
        wqkv = sb("wqkv", [P, 3, P])
        bqkv = sb("bqkv", [P, 3])
        w1, b1 = sb("w1", [P, PAIRS, P]), sb("b1", [P, 1])
        bproj, by = sb("bproj", [P, 1]), sb("by", [P, 1])
        scratch = sb("scratch", [P, PAIRS, P])

        xt = [sb(f"x{s}", [P, R, UW]) for s in range(2)]
        qk_split = sb("qk", [P, 4, HALVES * HALF], F16)
        q_sided = sb("q_sided", [P, 2, WIN, 2, TOK], F16)
        k_headed = sb("k_headed", [P, 2, WIN, HEADS, TOK], F16)
        ones = sb("ones", [P, WIN])
        x_twice = sb("x_twice", [P, WIN, HEADS, TOK])
        qs = [sb(f"qs{s}", [KROWS + TOPS, PAIRS, WIN * 2 * TOK], F16) for s in range(2)]
        ks = [sb(f"ks{s}", [KROWS + TOPS, PAIRS, WIN, HEADS * TOK], F16) for s in range(2)]
        vt = [sb(f"v{s}", [P, WIN, SB * C]) for s in range(2)]
        top = [sb(f"max{i}", [P, PAIRS * HEADS], BF16) for i in range(2)]
        eye16 = sb("eye16", [P, P], BF16)
        probs = [sb(f"probs{i}", [P, 512]) for i in range(3)]
        inv = [sb(f"inv{i}", [P, 2, TOK]) for i in range(2)]
        att_t = [sb(f"att_t{s}", [P, WIN, P]) for s in range(2)]
        z = sb("z", [P, HALVES, HALF])
        hid = sb("hid", [P, HALVES, PAIRS, HALF])
        yt = [sb(f"y{s}", [P, R, UW]) for s in range(2)]

        with ExitStack() as c2:
            sem2 = lambda name: c2.enter_context(nc.semaphore("prep_" + name))
            loaded, scaled, product, copied = (sem2(n) for n in ("loaded", "scaled", "product", "copied"))
            block = c2.enter_context(nc.Block())

            @block.sync
            def _(sp):
                for name, d in w_d.items():
                    sp.dma_start(w[name][tuple(slice(None) for _ in d.shape)], d).then_inc(loaded, 16)

            @block.gpsimd
            def _(pool):
                nc.gpsimd.memset(ones[:, :], 1.0)

            @block.vector
            def _(dve):
                dve.wait_ge(loaded, 16 * len(w_d))
                nc.vector.tensor_copy(eye16[:, :], w["eye"][:, :])
                for t in ks:
                    for p in range(PAIRS):
                        nc.vector.tensor_copy(
                            t[KROWS:, p, :, :].rearrange("k w (h n) -> k w h n", h=HEADS),
                            w["top_rows"][KROWS:KROWS + TOPS, p, :].unsqueeze(1).unsqueeze(3).to_broadcast(
                                [TOPS, WIN, HEADS, TOK]))
                cols = w["cols"]
                for i in range(3):
                    nc.vector.tensor_scalar(scratch[:, i, :], w["qkv"][:, i, :], cols[:, 0:1],
                                            HD ** -0.5 if i == 0 else 1.0, ALU.mult, ALU.mult).then_inc(scaled, 1)
                dve.wait_ge(product, 1)
                nc.vector.tensor_copy(wqkv[:, :, :], misc[0][:, 0:3 * P].rearrange("p (i c) -> p i c", i=3)).then_inc(copied, 1)
                nc.vector.tensor_tensor(bqkv[:, :], misc[1][:, 0:3], cols[:, 4:7], ALU.add).then_inc(copied, 1)
                dve.wait_ge(copied, 2)
                nc.vector.tensor_scalar(bqkv[:, 0:1], bqkv[:, 0:1], HD ** -0.5, None, ALU.mult).then_inc(copied, 1)
                for p in range(PAIRS):
                    nc.vector.tensor_scalar(scratch[:, p, :], w["fc1"][:, p, :], cols[:, 2:3], None, ALU.mult).then_inc(scaled, 1)
                dve.wait_ge(product, 2)
                nc.vector.tensor_copy(w1[:, :, :], misc[0][:, :].rearrange("p (i c) -> p i c", i=PAIRS)).then_inc(copied, 1)
                nc.vector.tensor_tensor(bproj[:, :], misc[1][:, 3:4], cols[:, 7:8], ALU.add).then_inc(copied, 1)
                dve.wait_ge(copied, 5)
                nc.vector.tensor_tensor(by[:, :], bproj[:, :], cols[:, 9:10], ALU.add).then_inc(copied, 1)
                dve.wait_ge(product, 3)
                nc.vector.tensor_tensor(b1[:, :], misc[1][:, 4:5], cols[:, 8:9], ALU.add).then_inc(copied, 1)

            @block.tensor
            def _(pe):
                pe.wait_ge(loaded, 16 * len(w_d))
                cols = w["cols"]
                for i in range(3):
                    nc.tensor.matmul(misc[1][:, i:i + 1], w["qkv"][:, i, :], cols[:, 1:2], start=True, stop=True)
                pe.wait_ge(scaled, 3)
                for i in range(3):
                    last = nc.tensor.matmul(misc[0][:, i * P:(i + 1) * P], w["color1"][:, :], scratch[:, i, :], start=True, stop=True)
                last.then_inc(product, 1)
                pe.wait_ge(copied, 3)
                pe.wait_ge(scaled, 3 + PAIRS)
                for a in range(2):
                    nc.tensor.matmul(misc[1][:, 3:4], w["proj"][:, a, :], bqkv[:, 2:3], start=(a == 0), stop=(a == 1))
                for p in range(PAIRS):
                    last = nc.tensor.matmul(misc[0][:, p * P:(p + 1) * P], w["color2"][:, :], scratch[:, p, :], start=True, stop=True)
                last.then_inc(product, 1)
                pe.wait_ge(copied, 5)
                nc.tensor.matmul(misc[1][:, 4:5], w["fc1"][:, 0, :], cols[:, 3:4], start=True, stop=False)
                nc.tensor.matmul(misc[1][:, 4:5], w1[:, 0, :], bproj[:, 0:1], start=False, stop=True).then_inc(product, 1)

        x_copied, placed_ready = sem("x_copied"), sem("placed_ready")
        x_in = [sem(f"x_in{s}") for s in range(2)]
        qk_parted = sem("qk_parted")
        qk_in = [sem(f"qk_in{s}") for s in range(2)]
        projected, qk_done, v_done, s_done, top_turned, t_done, pv_done = (sem(n) for n in (
            "projected", "qk_done", "v_done", "s_done", "top_turned", "t_done", "pv_done"))
        qk_high, v_ready, max_ready, top_placed, probs_ready, inv_ready, att_t_ready = (sem(n) for n in (
            "qk_high", "v_ready", "max_ready", "top_placed", "probs_ready", "inv_ready", "att_t_ready"))
        z_ready, fc1_done, hid_ready, fc2_done, y_ready = (sem(n) for n in ("z_ready", "fc1_done", "hid_ready", "fc2_done", "y_ready"))
        y_out = [sem(f"y_out{s}") for s in range(2)]
        block = ctx.enter_context(nc.Block())

        QK_MOVES = PARTS * PAIRS * 2
        LAST = UNITS + 1
        has_mlp = lambda u: within(u, 2, UNITS + 2)
        has_att = lambda u: within(u, 1, UNITS + 1)
        has_in = lambda u: within(u, 0, UNITS)

        def unit_at(sup, quarter):
            return lambda t: t[bass.ds(sup * SB + sup // (BPI // SB) + 1, SB)].rearrange(
                "b (c r) w -> (b c) r w", r=R)[:, :, bass.ds(quarter * UW, UW)]

        def run(eng, body, lag=0):
            for u in range(4):
                v = max(u - lag, 0)
                body(u, u % 2, unit_at(v // UPS, v % UPS))
            with eng.Fori(2, UNITS // 2) as k:
                m = k - lag // 2
                for s in range(2):
                    body(k * 2 + s, s, unit_at(m // 2, m % 2 * 2 + s))
            for u in range(UNITS, LAST + 1):
                v = u - lag
                body(u, u % 2, unit_at(v // UPS, v % UPS))

        @block.sync
        def _(sp):
            def move(u, s, window):
                if not has_in(u):
                    return
                if within(u, 2, UNITS):
                    sp.wait_ge(z_ready, HALVES * (u - 1))
                sp.dma_start(xt[s][:, :, :], window(x)).then_inc(x_in[s], 16)
                if within(u, 2, UNITS):
                    sp.wait_ge(t_done, WIN * (u - 1))
                for which, src, dst in ((1, k_headed, ks[s]), (0, q_sided, qs[s])):
                    sp.wait_ge(placed_ready, 8 * u + 8 - 4 * which)
                    for part in range(PARTS):
                        low = int(part == 1 + which)
                        for p in range(PAIRS):
                            stack = dst[part * 2 * C:(part + 1) * 2 * C, p]
                            sp.dma_start(stack.rearrange("k w n -> k (w n)") if which else stack,
                                         src[p * 2 * C:(p + 1) * 2 * C, low, :, :, :].rearrange("p w a n -> p (w a n)"))\
                                .then_inc(qk_in[s], 16)
            run(sp, move)

        @block.gpsimd
        def _(pool):
            def store(u, s, window):
                if has_in(u):
                    pool.wait_ge(x_in[s], (u // 2 + 1) * 16)
                    if within(u, 1, UNITS):
                        pool.wait_ge(v_done, 4 * u)
                    for h in range(HEADS):
                        nc.gpsimd.tensor_tensor(x_twice[:, :, h, :].rearrange("p w (r x) -> p w r x", x=WS),
                                                xt[s][:, :, :].rearrange("p r (w x) -> p w r x", x=WS),
                                                ones[:, :].unsqueeze(2).unsqueeze(3).to_broadcast([P, WIN, R, WS]),
                                                ALU.mult).then_inc(x_copied, 1)
                if has_mlp(u):
                    pool.wait_ge(y_ready, HALVES * (u - 1))
                    pool.dma_start(window(y), yt[s][:, :, :]).then_inc(y_out[s], 16)
            run(pool, store, lag=2)
            for s in range(2):
                pool.wait_ge(y_out[s], 16 * UNITS // 2)

        def columns(t, half):
            return t[:, :, half * HW_:(half + 1) * HW_]

        def by_window(t, half):
            return columns(t, half).rearrange("p r (w x) -> p w r x", x=WS)

        SLICES = WIN + 6
        PROJ, FC1, FC2, QK, V = {1: (0, 1)}, 2, {4: 0, 5: 1}, {6: 0, 7: 1, 8: 2, 9: 3}, {10: 0, 12: 1, 14: 2, 16: 3}
        PLACE = {8: (1, 0), 9: (1, 1), 10: (0, 0), 11: (0, 1)}
        qk_job = lambda q: (q % 2, 1 - q // 2)
        FC1_JOBS = HALVES * PAIRS
        NORMALIZED = WIN // 2
        normalize_at = lambda i: (i - 6) // 2 if i >= 6 and i % 2 == 0 and (i - 6) // 2 < NORMALIZED else None

        @block.tensor
        def _(pe):
            def mlp(u, s, i):
                c = u - 2
                for half in PROJ.get(i, ()):
                    pe.wait_ge(att_t_ready, NORMALIZED * (c + 1))
                    if has_in(u - 1):
                        pe.wait_ge(v_ready, 4 * u - 1 + half)
                    elif c > 0:
                        pe.wait_ge(y_ready, HALVES * c)
                    for a in range(2):
                        last = nc.tensor.matmul(misc[half][:, :], w["proj"][:, a, :],
                                                att_t[s][:, half * WPH:(half + 1) * WPH, a * TOK:(a + 1) * TOK],
                                                start=(a == 0), stop=(a == 1))
                    last.then_inc(projected, 1)
                for j in range(FC1_JOBS if i == FC1 else 0):
                    half, p = divmod(j, PAIRS)
                    if j < 2:
                        pe.wait_ge(z_ready, HALVES * c + j + 1)
                    else:
                        pe.wait_ge(hid_ready, FC1_JOBS * c + j - 1)
                    nc.tensor.matmul(misc[j % 2][:, :], w1[:, p, :], z[:, half, :], start=True, stop=True).then_inc(fc1_done, 1)
                if i in FC2:
                    half = FC2[i]
                    pe.wait_ge(hid_ready, FC1_JOBS * c + FC1_JOBS - 1 + half)
                    for p in range(PAIRS):
                        last = nc.tensor.matmul(misc[half][p * 2 * C:(p + 1) * 2 * C, :], w["fc2"][:, :],
                                                hid[:, half, p, :], start=True, stop=True)
                    last.then_inc(fc2_done, 1)

            def project(u, s, i):
                if i in QK:
                    q = QK[i]
                    half, which = qk_job(q)
                    if q == 0:
                        pe.wait_ge(x_in[s], (u // 2 + 1) * 16)
                    if q > 1:
                        pe.wait_ge(qk_parted, 4 * u + q - 1)
                    elif has_mlp(u):
                        pe.wait_ge(y_ready, HALVES * (u - 2) + q + 1)
                    elif u == 1:
                        pe.wait_ge(v_ready, 3 + q)
                    nc.tensor.matmul(misc[q % 2][:, :], wqkv[:, which, :], by_window(xt[s], half), start=True, stop=True)\
                        .then_inc(qk_done, 1)
                if i in V:
                    v = V[i]
                    if v == 0:
                        pe.wait_ge(x_copied, HEADS * (u + 1))
                    if v < 2:
                        pe.wait_ge(qk_parted, 4 * u + 3 + v)
                    else:
                        pe.wait_ge(v_ready, 4 * u + v - 1)
                    for j in range(4):
                        both = x_twice[:, 4 * v + j, :, :].rearrange("p h n -> p (h n)")
                        last = nc.tensor.matmul(misc[v % 2][:, j * P:(j + 1) * P], both, wqkv[:, 2, :], start=True, stop=True)
                    last.then_inc(v_done, 1)

            def attend(u, s, i):
                b = u - 1
                s = 1 - s
                if i == 0:
                    pe.wait_ge(qk_in[s], (b // 2 + 1) * 16 * QK_MOVES if isinstance(u, int) else
                               (8 * QK_MOVES * (b - s) + 16 * QK_MOVES))
                    pe.wait_ge(v_ready, 4 * b + 4)
                if i < WIN:
                    if within(u, 2, UNITS + 1) or i >= 2:
                        pe.wait_ge(top_placed, WIN * b + i - 1)
                    for p in range(PAIRS):
                        last = nc.tensor.matmul(scores[i % 2][:, p * P:(p + 1) * P], qs[s][0:KROWS, p, i * P:(i + 1) * P],
                                                ks[s][0:KROWS, p, i, :], start=True, stop=True)
                    last.then_inc(s_done, 1)
                if 1 <= i < WIN + 1:
                    j = i - 1
                    pe.wait_ge(max_ready, WIN * b + j + 1)
                    nc.tensor.matmul(scores[j % 2][KROWS:KROWS + TOPS, 0:P], top[j % 2][:, :],
                                     eye16[:, :], start=True, stop=True).then_inc(top_turned, 1)
                if 2 <= i < WIN + 2:
                    j = i - 2
                    pe.wait_ge(top_placed, WIN * b + j + 1)
                    if within(u, 2, UNITS + 1) or j >= 2:
                        pe.wait_ge(probs_ready, WIN * b + j - 1)
                    for p in range(PAIRS):
                        last = nc.tensor.matmul(scores_t[j % 2][:, p * P:(p + 1) * P], ks[s][:, p, j, :],
                                                qs[s][:, p, j * P:(j + 1) * P], start=True, stop=True)
                    last.then_inc(t_done, 1)
                if 4 <= i < WIN + 4:
                    j = i - 4
                    pe.wait_ge(probs_ready, WIN * b + j + 1)
                    if j % 2 == 0 and (within(u, 2, UNITS + 1) or j >= 4):
                        pe.wait_ge(att_t_ready, NORMALIZED * b + j // 2 - 1)
                    tile = weighted[j // 2 % 2]
                    rows = [slice(p * 2 * C, (p + 1) * 2 * C) for p in range(PAIRS)]
                    for p in range(PAIRS):
                        nc.tensor.matmul(tile[rows[p], j % 2 * P:(j % 2 + 1) * P], vt[s][:, j, rows[p]],
                                         probs[j % 3][:, p * P:(p + 1) * P], start=True, stop=True)
                    for a in range(2):
                        for p in range(PAIRS):
                            last = nc.tensor.matmul(tile[rows[p], 2 * P + j % 2 * TOK:2 * P + (j % 2 + 1) * TOK],
                                                    w["head_mask"][:, a, :],
                                                    probs[j % 3][:, (2 * p + a) * TOK:(2 * p + a + 1) * TOK],
                                                    start=(a == 0), stop=(a == 1))
                    last.then_inc(pv_done, 1)

            def step(u, s, _):
                for i in range(SLICES):
                    if has_att(u):
                        attend(u, s, i)
                    if has_mlp(u):
                        mlp(u, s, i)
                    if has_in(u):
                        project(u, s, i)
            run(pe, step)

        @block.scalar
        def _(act):
            def attend(u, s, i):
                b = u - 1
                if 1 <= i < WIN + 1:
                    j = i - 1
                    act.wait_ge(top_turned, WIN * b + j + 1)
                    nc.scalar.activation(qs[1 - s][KROWS:, :, j * P:(j + 1) * P],
                                         scores[j % 2][KROWS:KROWS + TOPS, 0:P].unsqueeze(1).to_broadcast([TOPS, PAIRS, P]),
                                         ACT.Copy, scale=1 / TOP_SCALE).then_inc(top_placed, 1)
                if 2 <= i < WIN + 2:
                    j = i - 2
                    act.wait_ge(t_done, WIN * b + j + 1)
                    if within(u, 2, UNITS + 1) or j >= 3:
                        act.wait_ge(pv_done, WIN * b + j - 2)
                    nc.scalar.activation(probs[j % 3][:, :], scores_t[j % 2][:, :], ACT.Exp).then_inc(probs_ready, 1)

            def step(u, s, _):
                for i in range(SLICES):
                    if has_att(u):
                        attend(u, s, i)
                    for j in range(FC1_JOBS if i == FC1 and has_mlp(u) else 0):
                        act.wait_ge(fc1_done, FC1_JOBS * (u - 2) + j + 1)
                        if within(u, 3, UNITS + 2) and j % PAIRS == 0:
                            act.wait_ge(fc2_done, HALVES * (u - 3) + j // PAIRS + 1)
                        nc.scalar.activation(hid[:, j // PAIRS, j % PAIRS, :], misc[j % 2][:, :], ACT.Gelu,
                                             bias=b1[:, 0:1]).then_inc(hid_ready, 1)
                    if i in QK and has_in(u):
                        half, which = qk_job(QK[i])
                        act.wait_ge(qk_done, 4 * u + QK[i] + 1)
                        if QK[i] == 0 and within(u, 1, UNITS):
                            act.wait_ge(placed_ready, 8 * u)
                        nc.scalar.activation(qk_split[:, 2 * which, half * HALF:(half + 1) * HALF], misc[QK[i] % 2][:, :],
                                             ACT.Identity, bias=bqkv[:, which:which + 1]).then_inc(qk_high, 1)
            run(act, step)

        @block.vector
        def _(dve):
            def mlp(u, s, i):
                c = u - 2
                for half in PROJ.get(i, ()):
                    dve.wait_ge(projected, HALVES * c + half + 1)
                    if within(u, 3, UNITS + 2) and half == 0:
                        dve.wait_ge(y_ready, HALVES * c)
                    nc.vector.tensor_tensor(
                        z[:, half, :].rearrange("p (r w x) -> p r w x", r=R, x=WS),
                        misc[half][:, :].rearrange("p (w r x) -> p r w x", r=R, x=WS),
                        columns(xt[s], half).rearrange("p r (w x) -> p r w x", x=WS), ALU.add).then_inc(z_ready, 1)
                if i in FC2:
                    half = FC2[i]
                    if half == 0 and within(u, 4, UNITS + 2):
                        dve.wait_ge(y_out[s], (8 * (u - s) - 16) if not isinstance(u, int) else 16 * (u // 2 - 1))
                    dve.wait_ge(fc2_done, HALVES * c + half + 1)
                    nc.vector.scalar_tensor_tensor(
                        columns(yt[s], half), misc[half][:, :].rearrange("p (r x) -> p r x", r=R), by[:, 0:1],
                        z[:, half, :].rearrange("p (r x) -> p r x", r=R), ALU.add, ALU.add).then_inc(y_ready, 1)

            def project(u, s, i):
                if i in QK:
                    half, which = qk_job(QK[i])
                    high = qk_split[:, 2 * which, half * HALF:(half + 1) * HALF]
                    low = qk_split[:, 2 * which + 1, half * HALF:(half + 1) * HALF]
                    dve.wait_ge(qk_high, 4 * u + QK[i] + 1)
                    nc.vector.scalar_tensor_tensor(low, misc[QK[i] % 2][:, :], bqkv[:, which:which + 1], high,
                                                   ALU.add, ALU.subtract).then_inc(qk_parted, 1)
                if i in PLACE:
                    which, part = PLACE[i]
                    dst, marks = ((q_sided, w["sides"]), (k_headed, w["key_heads"]))[which]
                    dve.wait_ge(qk_parted, 4 * u + 4 - 2 * which)
                    if part == 0 and within(u, 2, UNITS):
                        dve.wait_ge(qk_in[1 - s], 8 * QK_MOVES * (u - s) + s * 16 * QK_MOVES if not isinstance(u, int)
                                    else 16 * QK_MOVES * ((u + 1) // 2))
                    elif part == 0 and u == 1:
                        dve.wait_ge(qk_in[0], 16 * QK_MOVES)
                    for copy in range(2):
                        nc.vector.tensor_scalar(dst[:, part, :, copy, :],
                                                qk_split[:, 2 * which + part, :].rearrange("p (w n) -> p w n", n=TOK),
                                                marks[:, copy:copy + 1], None, ALU.mult).then_inc(placed_ready, 1)
                if i in V:
                    dve.wait_ge(v_done, 4 * u + V[i] + 1)
                    if V[i] == 0 and within(u, 2, UNITS):
                        dve.wait_ge(pv_done, WIN * (u - 1))
                    nc.vector.tensor_tensor(vt[s][:, 4 * V[i]:4 * V[i] + 4, :].rearrange("p w (g c) -> p (w g) c", c=C),
                                            misc[V[i] % 2][:, :].rearrange("p (w c) -> p w c", c=C),
                                            w["head_mask"][:, 0, 0:C].unsqueeze(1).to_broadcast([P, 4 * SB, C]),
                                            ALU.mult).then_inc(v_ready, 1)

            def attend(u, s, i):
                b = u - 1
                if i < WIN:
                    dve.wait_ge(s_done, WIN * b + i + 1)
                    if within(u, 2, UNITS + 1) or i >= 2:
                        dve.wait_ge(top_turned, WIN * b + i - 1)
                    nc.vector.tensor_reduce(top[i % 2][:, :], scores[i % 2][:, :].rearrange("p (k m) -> p k m", m=TOK),
                                            AX.X, ALU.max).then_inc(max_ready, 1)
                j = normalize_at(i)
                if j is not None:
                    dve.wait_ge(pv_done, WIN * b + 2 * j + 2)
                    sums = weighted[j % 2][:, 2 * P:2 * P + 2 * TOK].rearrange("p (w n) -> p w n", w=2)
                    nc.vector.reciprocal(inv[j % 2][:, :, :], sums).then_inc(inv_ready, 1)
                    dve.wait_ge(inv_ready, NORMALIZED * b + j + 1)
                    if j == 0 and within(u, 3, UNITS + 1):
                        dve.wait_ge(projected, HALVES * (u - 2))
                    nc.vector.tensor_tensor(att_t[1 - s][:, 2 * j:2 * j + 2, :].rearrange("p w (a n) -> p w a n", a=2),
                                            weighted[j % 2][:, 0:2 * P].rearrange("p (w a n) -> p w a n", w=2, a=2),
                                            inv[j % 2][:, :, :].unsqueeze(2).to_broadcast([P, 2, 2, TOK]),
                                            ALU.mult).then_inc(att_t_ready, 1)

            def step(u, s, _):
                for i in range(SLICES):
                    if has_att(u):
                        attend(u, s, i)
                    if has_mlp(u):
                        mlp(u, s, i)
                    if has_in(u):
                        project(u, s, i)
            run(dve, step)


def program(nc, x, pos_taps, eye, pos_b, taps, conv_b, color1, qkv, proj, color2, fc1, fc2, cols, head_mask, sides,
            key_heads, top_rows, out):
    dram = lambda name, shape, dt=F32: nc.dram_tensor(name, shape, dt, kind="Internal").ap()
    y = [dram(f"y{i}", [PB, P, W]) for i in range(4)]
    edges_x = dram("edges_x", [2, PB, C, W])
    h_edges = [dram(f"edges_h{i}", [2, PB, C, W]) for i in range(3)]
    zero_borders(nc, y, [edges_x] + h_edges)
    position_conv(nc, x, pos_taps, eye, pos_b, edges_x, y[0])
    attention_mlp(nc, dict(color1=color1, qkv=qkv, proj=proj, color2=color2, fc1=fc1, fc2=fc2, cols=cols,
                           head_mask=head_mask, sides=sides, key_heads=key_heads, top_rows=top_rows, eye=eye),
                  y[0], y[1])
    for i in range(3):
        residual_pair(nc, f"layer{i + 1}", taps[2 * i], taps[2 * i + 1], conv_b[2 * i], conv_b[2 * i + 1],
                      y[i + 1], i == 0, out if i == 2 else y[i + 2], i == 2, h_edges[i])


_ORDER = ["x", "pos_taps", "eye", "pos_b", "taps", "conv_b", "color1", "qkv", "proj", "color2", "fc1", "fc2", "cols",
          "head_mask", "sides", "key_heads", "top_rows"]


def kernel(**inputs):
    import numpy as np
    import concourse.bacc as _bacc
    from concourse import mybir as _mybir
    from concourse.bass_utils import run_bass_kernel_spmd as _run

    def banded(w):
        t = np.zeros((P, TAPS + 1, P), np.float32)
        for r in range(R):
            cols = slice(r * C, (r + 1) * C)
            for ky in range(3):
                for kx in range(3):
                    r_in, m = r + ky - 1, w[:, :, ky, kx].T
                    if 0 <= r_in < R:
                        t[r_in * C:(r_in + 1) * C, kx, cols] = m
                    else:
                        p0 = (kx * 2 + (r_in == R)) * C
                        t[p0:p0 + C, TAPS, cols] = m
        return t

    a = {k: np.asarray(v) for k, v in inputs.items()}
    depthwise = np.zeros((C, C, 3, 3), np.float32)
    depthwise[np.arange(C), np.arange(C)] = a["L0_conv_pos_w"][:, 0]
    arrays = {"x": np.ascontiguousarray(a["x"]), "pos_taps": banded(depthwise), "eye": np.eye(P, dtype=np.float32),
              "pos_b": np.tile(a["L0_conv_pos_b"], R).reshape(P, 1),
              "taps": np.stack([banded(a[f"L{i}_conv_w{j}"]) for i in (1, 2, 3) for j in (1, 2)]),
              "conv_b": np.stack([np.tile(a[f"L{i}_conv_b{j}"], R).reshape(P, 1) for i in (1, 2, 3) for j in (1, 2)])}

    def diagonal(m, blocks=range(SB)):
        t = np.zeros((P, P), np.float32)
        for g in blocks:
            t[g * C:(g + 1) * C, g * C:(g + 1) * C] = m
        return t

    fc1, fc2 = np.zeros((P, PAIRS, P), np.float32), np.zeros((P, 2 * C), np.float32)
    for side in range(2):
        fc2[side * HID:(side + 1) * HID, side * C:(side + 1) * C] = a["L0_conv_fc2_w"].T
    for p in range(PAIRS):
        for side in range(2):
            g = 2 * p + side
            fc1[g * C:(g + 1) * C, p, side * HID:(side + 1) * HID] = a["L0_conv_fc1_w"].T
    qkv_w, qkv_b = a["L0_conv_qkv_w"], a["L0_conv_qkv_b"]
    column = lambda v: np.tile(v.reshape(-1), P // v.size)
    mask = np.zeros((P, 2, 2 * C), np.float32)
    for side in range(2):
        for h in range(HEADS):
            mask[h * TOK:(h + 1) * TOK, side, side * C + h * HD:side * C + (h + 1) * HD] = 1.0
    top_rows = np.zeros((P, PAIRS, HEADS), np.float32)
    top_rows[KROWS + np.arange(PAIRS * HEADS)] = -TOP_SCALE * np.eye(PAIRS * HEADS).reshape(-1, PAIRS, HEADS)
    arrays.update(
        color1=diagonal(a["L0_conv_color1"]), color2=diagonal(a["L0_conv_color2"]),
        qkv=np.stack([diagonal(qkv_w[i * C:(i + 1) * C].T) for i in range(3)], axis=1),
        proj=np.stack([diagonal(a["L0_conv_proj_w"].T, range(side, SB, 2)) for side in range(2)], axis=1),
        fc1=fc1, fc2=fc2, head_mask=mask,
        sides=np.repeat(np.tile(np.eye(2, dtype=np.float32), (PAIRS, 1)), C, axis=0),
        key_heads=np.repeat(np.tile(np.eye(HEADS, dtype=np.float32), (SB, 1)), HD, axis=0), top_rows=top_rows,
        cols=np.stack([column(v) for v in (
            a["L0_conv_alpha1"], a["L0_conv_beta1"], a["L0_conv_alpha2"], a["L0_conv_beta2"],
            qkv_b[0:C], qkv_b[C:2 * C], qkv_b[2 * C:], a["L0_conv_proj_b"], a["L0_conv_fc1_b"], a["L0_conv_fc2_b"])], axis=1))
    nc = _bacc.Bacc("TRN2", target_bir_lowering=False, num_devices=1)
    args = [nc.dram_tensor("in_" + k, arrays[k].shape, _mybir.dt.from_np(arrays[k].dtype), kind="ExternalInput").ap()
            for k in _ORDER]
    args.append(nc.dram_tensor("out", (IMAGES, C, H, W), F32, kind="ExternalOutput").ap())
    program(nc, *args)
    r = _run(nc, [{"in_" + k: v for k, v in arrays.items()}], core_ids=[0])
    return r.results[0]["out"]
```

```python
from contextlib import ExitStack

import concourse.bass as bass
from concourse import mybir

F32 = mybir.dt.float32
F16 = mybir.dt.float16
ACT = mybir.ActivationFunctionType
ALU = mybir.AluOpType
AX = mybir.AxisListType

P = 128
C = 16
R = 8
TAPS = 3
IMAGES, H, W = 4, 512, 512
BPI = H // R
NB = 4
GROUPS = IMAGES * BPI // NB
GPI = BPI // NB
PB = IMAGES * (BPI + 1) + 1
WP = W + 2
EDGE = TAPS * 2 * C
UNROLL = 4
LAG = 2


def padded(g):
    return g * NB + g // GPI


def clear_borders(nc, tiles, cleared):
    for tile in tiles:
        for c0 in (0, W):
            nc.gpsimd.memset(tile[:, :, c0:c0 + 2], 0.0).then_inc(cleared, 1)


def load_edges(q, tile, above, below, g, done, parts=False):
    for tap in range(TAPS):
        for t, src, skip in ((0, above, 0), (1, below, 2)):
            p0 = (tap * 2 + t) * C
            blocks, x = bass.ds(padded(g) + skip, NB), slice(TAPS - 1 - tap, TAPS - 1 - tap + W)
            if parts:
                q.dma_start(tile[p0:p0 + C, :, :, x], src[:, blocks, :, :]).then_inc(done, 16)
            else:
                q.dma_start(tile[p0:p0 + C, :, x], src[:, blocks, :]).then_inc(done, 16)


EDGE_LOADS = 2 * TAPS


def convolve(nc, out, taps, x, edge, edge_wait):
    for tap in range(TAPS):
        for wpart, part in PRODUCTS:
            for n in range(NB):
                nc.tensor.matmul(out[n][:, :], taps[:, wpart, tap, :], x[:, n, part, tap:tap + W],
                                 start=(tap == 0 and wpart == part == 0), stop=False)
    edge_wait()
    for i, (wpart, part) in enumerate(PRODUCTS):
        for n in range(NB):
            last = nc.tensor.matmul(out[n][:, :], taps[0:EDGE, wpart, TAPS, :], edge[:, n, part, 1:1 + W],
                                    start=False, stop=(i == len(PRODUCTS) - 1))
    return last


PRODUCTS = ((0, 0), (0, 1), (1, 0))


def split_taps(nc, dve, taps, parts, done, done_before):
    nc.vector.tensor_copy(parts[:, 0, :, :], taps[:, :, :]).then_inc(done, 1)
    dve.wait_ge(done, done_before + 1)
    nc.vector.tensor_tensor(parts[:, 1, :, :], taps[:, :, :], parts[:, 0, :, :], ALU.subtract).then_inc(done, 1)


def within(t, first, end):
    return not isinstance(t, int) or first <= t < end


def steps(eng, body, last_step):
    for t in range(UNROLL):
        body(t, t, t // 2)
    rounds = GROUPS // UNROLL
    with eng.Fori(1, rounds) as k:
        for u in range(UNROLL):
            body(k * UNROLL + u, u, k * (UNROLL // 2) + u // 2)
    for t in range(GROUPS, last_step + 1):
        body(t, t % UNROLL, t // 2)


def zero_borders(nc, padded_tensors, edge_tensors, edge_parts):
    with ExitStack() as ctx:
        zeros = ctx.enter_context(nc.sbuf_tensor("zeros", [P, IMAGES + 1, W], F32))
        zeros16 = ctx.enter_context(nc.sbuf_tensor("zeros16", [C, IMAGES + 1, W], F16))
        zeroed = ctx.enter_context(nc.semaphore("zeroed"))
        stored = ctx.enter_context(nc.semaphore("borders_stored"))
        block = ctx.enter_context(nc.Block())

        @block.vector
        def _(dve):
            nc.vector.memset(zeros[:, :, :], 0.0).then_inc(zeroed, 1)
            nc.vector.memset(zeros16[:, :, :], 0.0).then_inc(zeroed, 1)

        @block.sync
        def _(sp):
            sp.wait_ge(zeroed, 2)
            n = 0
            for t in padded_tensors:
                sp.dma_start(t.rearrange("b p x -> p b x")[:, ::BPI + 1, :], zeros[:, :, :]).then_inc(stored, 16)
                n += 1
            for e, zero in [(e, zeros) for e in edge_tensors] + [(e[:, :, part], zeros16) for e in edge_parts for part in range(2)]:
                for which in range(2):
                    sp.dma_start(e[which].rearrange("b c x -> c b x")[:, ::BPI + 1, :],
                                 zero[0:C, :, :]).then_inc(stored, 16)
                    n += 1
            sp.wait_ge(stored, 16 * n)


def position_conv(nc, x, taps_d, center_d, bias_d, edges, y):
    with ExitStack() as ctx:
        sb = lambda name, shape, dt=F32: ctx.enter_context(nc.sbuf_tensor(name, shape, dt))
        sem = lambda name: ctx.enter_context(nc.semaphore(name))
        taps = sb("pos_taps", [P, TAPS + 1, P])
        center = sb("pos_center", [P, P])
        bias = sb("pos_bias", [P, 1])
        xt = [sb(f"pos_x{s}", [P, NB, WP]) for s in range(UNROLL)]
        et = [sb(f"pos_edge{s}", [EDGE, NB, WP]) for s in range(2)]
        taps_parts = sb("pos_taps_parts", [P, 2, TAPS + 1, P], F16)
        x_parts = [sb(f"pos_x_parts{s}", [P, NB, 2, WP], F16) for s in range(2)]
        edge_parts = [sb(f"pos_edge_parts{s}", [EDGE, NB, 2, WP], F16) for s in range(2)]
        yt = [sb(f"pos_y{s}", [P, NB, W]) for s in range(2)]
        ps = [[ctx.enter_context(nc.psum_tensor(f"pos_ps{s}_{n}", [P, W], F32)) for n in range(NB)] for s in range(2)]
        weights_in, weights_ready, cleared, edges_made = sem("p_win"), sem("p_wready"), sem("p_clear"), sem("p_edges")
        x_in = [sem(f"p_x_in{s}") for s in range(UNROLL)]
        e_in = [sem(f"p_e_in{s}") for s in range(2)]
        high, low = sem("p_high"), sem("p_low")
        conv_done, y_ready = sem("p_conv"), sem("p_y")
        y_out = [sem(f"p_y_out{s}") for s in range(2)]
        block = ctx.enter_context(nc.Block())

        @block.sync
        def _(sp):
            sp.dma_start(taps[:, :, :], taps_d).then_inc(weights_in, 16)
            sp.dma_start(center[:, :], center_d).then_inc(weights_in, 16)
            sp.dma_start(bias[:, :], bias_d).then_inc(weights_in, 16)
            for which, row in ((0, 0), (1, R - 1)):
                for b in range(IMAGES):
                    at = b * (BPI + 1) + 1
                    sp.dma_start(edges[which, at:at + BPI].rearrange("i c w -> i c w"),
                                 x[b].rearrange("c (i r) w -> r i c w", r=R)[row]).then_inc(edges_made, 16)
            sp.wait_ge(cleared, 2 * (UNROLL + 2))

            def load(t, s, half):
                if isinstance(t, int) and t >= GROUPS:
                    return
                if not isinstance(t, int) or t >= UNROLL:
                    sp.wait_ge(low, 2 * (t - UNROLL + 1))
                for r in range(R):
                    src = x.rearrange("b c h w -> c b (h w)")
                    off = (t % GPI) * (NB * R * W)
                    win = src[:, t // GPI, bass.ds(off, NB * R * W)]
                    win = win.rearrange("c (n r w) -> r c n w", r=R, w=W)[r]
                    sp.dma_start(xt[s][r * C:(r + 1) * C, :, 1:1 + W], win).then_inc(x_in[s], 16)
                if isinstance(t, int) and t == 0:
                    sp.wait_ge(edges_made, 16 * 2 * IMAGES)
                if within(t, 2, GROUPS):
                    sp.wait_ge(low, 2 * (t - 1))
                load_edges(sp, et[s % 2], edges[1].rearrange("b c w -> c b w"),
                           edges[0].rearrange("b c w -> c b w"), t, e_in[s % 2])
            steps(sp, load, GROUPS - 1)

        @block.gpsimd
        def _(pool):
            clear_borders(nc, xt + et, cleared)
            def store(t, s, half):
                pool.wait_ge(y_ready, (t + 1))
                for r in range(R):
                    dst = y.rearrange("b (c r) w -> r c b w", r=R)[r][:, bass.ds(padded(t) + 1, NB), :]
                    pool.dma_start(dst, yt[s % 2][r * C:(r + 1) * C, :, :]).then_inc(y_out[s % 2], 16)
            steps(pool, store, GROUPS - 1)
            for s in range(2):
                pool.wait_ge(y_out[s], 16 * R * GROUPS // 2)

        @block.vector
        def _(dve):
            dve.wait_ge(weights_in, 48)
            nc.vector.tensor_tensor(taps[:, 1, :], taps[:, 1, :], center[:, :], ALU.add).then_inc(weights_ready, 1)
            dve.wait_ge(weights_ready, 1)
            split_taps(nc, dve, taps, taps_parts, weights_ready, 1)

            def lows(t, s, half):
                for i, (src, parts) in enumerate(((xt[s], x_parts[s % 2]), (et[s % 2], edge_parts[s % 2]))):
                    dve.wait_ge(high, 2 * t + i + 1)
                    nc.vector.tensor_tensor(parts[:, :, 1, :], src[:, :, :], parts[:, :, 0, :], ALU.subtract).then_inc(low, 1)
            steps(dve, lows, GROUPS - 1)

        @block.tensor
        def _(pe):
            pe.wait_ge(weights_ready, 3)
            def conv(t, s, half):
                pe.wait_ge(low, 2 * t + 1)
                if not isinstance(t, int) or t >= 2:
                    pe.wait_ge(y_ready, t - 1)
                convolve(nc, ps[s % 2], taps_parts, x_parts[s % 2], edge_parts[s % 2],
                         lambda: pe.wait_ge(low, 2 * t + 2)).then_inc(conv_done, 1)
            steps(pe, conv, GROUPS - 1)

        @block.scalar
        def _(act):
            act.wait_ge(weights_in, 48)
            def evacuate(t, s, half):
                if within(t, 0, GROUPS):
                    act.wait_ge(x_in[s], (t // UNROLL + 1) * 16 * R)
                    if within(t, 2, GROUPS):
                        act.wait_ge(conv_done, t - 1)
                    nc.scalar.copy(x_parts[s % 2][:, :, 0, :], xt[s][:, :, :]).then_inc(high, 1)
                    act.wait_ge(e_in[s % 2], (half + 1) * 16 * EDGE_LOADS)
                    nc.scalar.copy(edge_parts[s % 2][:, :, 0, :], et[s % 2][:, :, :]).then_inc(high, 1)
                if within(t, 1, GROUPS + 1):
                    gs = (s - 1) % 2
                    act.wait_ge(conv_done, t)
                    if within(t, 3, GROUPS + 1):
                        act.wait_ge(y_out[gs], (half - (1 - s % 2)) * 16 * R)
                    for n in range(NB):
                        last = nc.scalar.activation(yt[gs][:, n, :], ps[gs][n][:, :], ACT.Identity, bias=bias[:, 0:1])
                    last.then_inc(y_ready, 1)
            steps(act, evacuate, GROUPS)


def residual_pair(nc, name, taps1_d, taps2_d, b1_d, b2_d, src, src_rows_inner, dst, dst_image, h_edges):
    with ExitStack() as ctx:
        sb = lambda what, shape, dt=F32: ctx.enter_context(nc.sbuf_tensor(f"{name}_{what}", shape, dt))
        sem = lambda what: ctx.enter_context(nc.semaphore(f"{name}_{what}"))
        taps1, taps2 = sb("taps1", [P, TAPS + 1, P]), sb("taps2", [P, TAPS + 1, P])
        parts1, parts2 = (sb(f"taps_parts{i}", [P, 2, TAPS + 1, P], F16) for i in range(2))
        b1, b2 = sb("b1", [P, 1]), sb("b2", [P, 1])
        xt = [sb(f"x{s}", [P, NB, WP]) for s in range(UNROLL)]
        x_parts = [sb(f"x_parts{s}", [P, NB, 2, WP], F16) for s in range(2)]
        xe = [sb(f"x_edge{s}", [EDGE, NB, WP]) for s in range(2)]
        xe_parts = [sb(f"x_edge_parts{s}", [EDGE, NB, 2, WP], F16) for s in range(2)]
        hidden = [sb(f"hidden{s}", [P, NB, W]) for s in range(2)]
        h_parts = [sb(f"h_parts{s}", [P, NB, 2, WP], F16) for s in range(UNROLL)]
        he_parts = [sb(f"h_edge_parts{s}", [EDGE, NB, 2, WP], F16) for s in range(2)]
        yt = [sb(f"y{s}", [P, NB, W]) for s in range(2)]
        ps1 = [ctx.enter_context(nc.psum_tensor(f"{name}_ps1_{n}", [P, W], F32)) for n in range(NB)]
        ps2 = [ctx.enter_context(nc.psum_tensor(f"{name}_ps2_{n}", [P, W], F32)) for n in range(NB)]
        weights_in, cleared = sem("weights_in"), sem("cleared")
        x_in, xe_in = [sem(f"x_in{s}") for s in range(UNROLL)], [sem(f"xe_in{s}") for s in range(2)]
        x_high, x_low, taps_split = sem("x_high"), sem("x_low"), sem("taps_split")
        h_high, h_low = sem("h_high"), sem("h_low")
        he_in = [sem(f"he_in{s}") for s in range(2)]
        conv1_done, h_ready = sem("conv1_done"), sem("h_ready")
        h_edges_out = [sem(f"h_edges_out{s}") for s in range(UNROLL)]
        conv2_done, y_ready = sem("conv2_done"), sem("y_ready")
        y_out = [sem(f"y_out{s}") for s in range(2)]
        CLEARED = 2 * (UNROLL + 2 + 2 * UNROLL + 2 * 2)
        x_loads = R if src_rows_inner else 1
        y_stores = R if dst_image else 1
        block = ctx.enter_context(nc.Block())

        @block.sync
        def _(sp):
            for tile, d in ((taps1[:, :, :], taps1_d), (taps2[:, :, :], taps2_d), (b1[:, :], b1_d), (b2[:, :], b2_d)):
                sp.dma_start(tile, d).then_inc(weights_in, 16)
            sp.wait_ge(cleared, CLEARED)
            if src_rows_inner:
                above, below = (src.rearrange("b (c r) w -> r c b w", r=R)[r] for r in (R - 1, 0))
            else:
                above, below = (src.rearrange("b (r c) w -> r c b w", r=R)[r] for r in (R - 1, 0))

            def load(t, s, half):
                if within(t, 0, GROUPS):
                    if within(t, UNROLL, GROUPS):
                        sp.wait_ge(y_ready, t - UNROLL + 1)
                    blocks = bass.ds(padded(t) + 1, NB)
                    if src_rows_inner:
                        for r in range(R):
                            sp.dma_start(xt[s][r * C:(r + 1) * C, :, 1:1 + W],
                                         src.rearrange("b (c r) w -> r c b w", r=R)[r][:, blocks, :]).then_inc(x_in[s], 16)
                    else:
                        sp.dma_start(xt[s][:, :, 1:1 + W], src[blocks].rearrange("b p w -> p b w")).then_inc(x_in[s], 16)
                    if within(t, 2, GROUPS):
                        sp.wait_ge(x_low, 2 * (t - 1))
                    load_edges(sp, xe[s % 2], above, below, t, xe_in[s % 2])
                if within(t, LAG, GROUPS + LAG):
                    if within(t, 0, LAG + 1) and isinstance(t, int):
                        sp.wait_ge(h_edges_out[0], 32)
                    if within(t, LAG, GROUPS + 1):
                        sp.wait_ge(h_edges_out[(s - 1) % UNROLL], 32 * (t // UNROLL + (s > 0)))
                    if within(t, LAG + 2, GROUPS + LAG):
                        sp.wait_ge(conv2_done, t - LAG - 1)
                    load_edges(sp, he_parts[s % 2], h_edges[1].rearrange("b a c w -> c b a w"),
                               h_edges[0].rearrange("b a c w -> c b a w"), t - LAG, he_in[s % 2], parts=True)
            steps(sp, load, GROUPS + LAG - 1)

        @block.gpsimd
        def _(pool):
            clear_borders(nc, xt + xe + [t[:, :, part, :] for t in h_parts + he_parts for part in range(2)], cleared)
            pool.wait_ge(cleared, CLEARED)

            def move(t, s, half):
                if within(t, 0, GROUPS):
                    pool.wait_ge(h_low, t + 1)
                    for which, p0 in ((0, 0), (1, P - C)):
                        pool.dma_start(h_edges[which].rearrange("b a c w -> c b a w")[:, bass.ds(padded(t) + 1, NB), :, :],
                                       h_parts[s][p0:p0 + C, :, :, 1:1 + W]).then_inc(h_edges_out[s], 16)
                if within(t, 3, GROUPS + 3):
                    g, gs = t - 3, (s - 3) % 2
                    pool.wait_ge(y_ready, t - 2)
                    if dst_image:
                        image = dst.rearrange("b c h w -> c b (h w)")[:, g // GPI, bass.ds(g % GPI * (NB * R * W), NB * R * W)]
                        image = image.rearrange("c (n r w) -> r c n w", r=R, w=W)
                        for r in range(R):
                            pool.dma_start(image[r], yt[gs][r * C:(r + 1) * C, :, :]).then_inc(y_out[gs], 16)
                    else:
                        pool.dma_start(dst[bass.ds(padded(g) + 1, NB)].rearrange("b p w -> p b w"),
                                       yt[gs][:, :, :]).then_inc(y_out[gs], 16)
            steps(pool, move, GROUPS + 2)
            for s in range(2):
                pool.wait_ge(y_out[s], 16 * y_stores * GROUPS // 2)

        @block.tensor
        def _(pe):
            pe.wait_ge(taps_split, 4)

            def conv(t, s, half):
                if within(t, 0, GROUPS):
                    pe.wait_ge(x_low, 2 * t + 1)
                    if within(t, 1, GROUPS):
                        pe.wait_ge(h_ready, t)
                    convolve(nc, ps1, parts1, x_parts[s % 2], xe_parts[s % 2],
                             lambda: pe.wait_ge(x_low, 2 * t + 2)).then_inc(conv1_done, 1)
                if within(t, LAG, GROUPS + LAG):
                    gs = (s - LAG) % UNROLL
                    pe.wait_ge(h_low, t - LAG + 1)
                    if within(t, LAG + 1, GROUPS + LAG):
                        pe.wait_ge(y_ready, t - LAG)
                    convolve(nc, ps2, parts2, h_parts[gs], he_parts[gs % 2],
                             lambda: pe.wait_ge(he_in[gs % 2], half * 16 * EDGE_LOADS)).then_inc(conv2_done, 1)
            steps(pe, conv, GROUPS + LAG - 1)

        @block.scalar
        def _(act):
            act.wait_ge(weights_in, 64)
            act.wait_ge(cleared, CLEARED)

            def highs(t, s, half):
                if within(t, 1, GROUPS + 1):
                    gs = (s - 1) % UNROLL
                    act.wait_ge(conv1_done, t)
                    if within(t, 3, GROUPS + 1):
                        act.wait_ge(h_low, t - 2)
                    for n in range(NB):
                        last = nc.scalar.activation(hidden[gs % 2][:, n, :], ps1[n][:, :], ACT.Relu, bias=b1[:, 0:1])
                    last.then_inc(h_ready, 1)
                    act.wait_ge(h_ready, t)
                    if within(t, UNROLL + 1, GROUPS + 1):
                        act.wait_ge(conv2_done, t - UNROLL)
                        act.wait_ge(h_edges_out[gs], 32 // UNROLL * (t - (s or UNROLL)))
                    nc.scalar.copy(h_parts[gs][:, :, 0, 1:1 + W], hidden[gs % 2][:, :, :]).then_inc(h_high, 1)
                if within(t, 0, GROUPS):
                    act.wait_ge(x_in[s], (t // UNROLL + 1) * 16 * x_loads)
                    if within(t, 2, GROUPS):
                        act.wait_ge(conv1_done, t - 1)
                    nc.scalar.copy(x_parts[s % 2][:, :, 0, :], xt[s][:, :, :]).then_inc(x_high, 1)
                    act.wait_ge(xe_in[s % 2], (half + 1) * 16 * EDGE_LOADS)
                    nc.scalar.copy(xe_parts[s % 2][:, :, 0, :], xe[s % 2][:, :, :]).then_inc(x_high, 1)
            steps(act, highs, GROUPS)

        @block.vector
        def _(dve):
            dve.wait_ge(weights_in, 64)
            dve.wait_ge(cleared, CLEARED)

            split_taps(nc, dve, taps1, parts1, taps_split, 0)
            split_taps(nc, dve, taps2, parts2, taps_split, 2)

            def residual(t, s, half):
                if within(t, 1, GROUPS + 1):
                    gs = (s - 1) % UNROLL
                    dve.wait_ge(h_high, t)
                    nc.vector.tensor_tensor(h_parts[gs][:, :, 1, 1:1 + W], hidden[gs % 2][:, :, :],
                                            h_parts[gs][:, :, 0, 1:1 + W], ALU.subtract).then_inc(h_low, 1)
                if within(t, 0, GROUPS):
                    for i, (whole, parts) in enumerate(((xt[s], x_parts[s % 2]), (xe[s % 2], xe_parts[s % 2]))):
                        dve.wait_ge(x_high, 2 * t + i + 1)
                        nc.vector.tensor_tensor(parts[:, :, 1, :], whole[:, :, :], parts[:, :, 0, :],
                                                ALU.subtract).then_inc(x_low, 1)
                if within(t, LAG + 1, GROUPS + LAG + 1):
                    gs = (s - LAG - 1) % UNROLL
                    dve.wait_ge(conv2_done, t - LAG)
                    if within(t, LAG + 3, GROUPS + LAG + 1):
                        dve.wait_ge(y_out[gs % 2], (half - 2 + s % 2) * 16 * y_stores)
                    for n in range(NB):
                        last = nc.vector.scalar_tensor_tensor(yt[gs % 2][:, n, :], ps2[n][:, :], b2[:, 0:1],
                                                              xt[gs][:, n, 1:1 + W], ALU.add, ALU.add)
                    last.then_inc(y_ready, 1)
            steps(dve, residual, GROUPS + LAG)


SB = P // C
WS = 8
TOK = WS * WS
PAIRS = SB // 2
UW = 128
WIN = UW // WS
UPS = W // UW
UNITS = IMAGES * BPI // SB * UPS
HALF = 512
HALVES = 2
HW_ = UW // HALVES
WPH = WIN // HALVES
HEADS, HD = 2, C // 2
HID = 64
PARTS = 3
KROWS = PARTS * 2 * C
TOPS = PAIRS * HEADS
TOP_SCALE = 1024.0
BF16 = mybir.dt.bfloat16


def attention_mlp(nc, w_d, x, y):
    with ExitStack() as ctx:
        sb = lambda name, shape, dt=F32: ctx.enter_context(nc.sbuf_tensor("at_" + name, shape, dt))
        sem = lambda name: ctx.enter_context(nc.semaphore("at_" + name))
        bank = lambda name: ctx.enter_context(nc.psum_tensor("at_ps_" + name, [P, 512], F32))
        scores, scores_t, weighted, misc = ([bank(f"{n}{i}") for i in range(2)] for n in ("s", "t", "o", "m"))

        w = {name: sb(name, list(d.shape)) for name, d in w_d.items()}
        wqkv = sb("wqkv", [P, 3, P])
        bqkv = sb("bqkv", [P, 3])
        w1, b1 = sb("w1", [P, PAIRS, P]), sb("b1", [P, 1])
        bproj, by = sb("bproj", [P, 1]), sb("by", [P, 1])
        scratch = sb("scratch", [P, PAIRS, P])

        xt = [sb(f"x{s}", [P, R, UW]) for s in range(2)]
        qk_split = sb("qk", [P, 4, HALVES * HALF], F16)
        q_sided = sb("q_sided", [P, 2, WIN, 2, TOK], F16)
        k_headed = sb("k_headed", [P, 2, WIN, HEADS, TOK], F16)
        ones = sb("ones", [P, WIN])
        x_twice = sb("x_twice", [P, WIN, HEADS, TOK])
        qs = [sb(f"qs{s}", [KROWS + TOPS, PAIRS, WIN * 2 * TOK], F16) for s in range(2)]
        ks = [sb(f"ks{s}", [KROWS + TOPS, PAIRS, WIN, HEADS * TOK], F16) for s in range(2)]
        vt = [sb(f"v{s}", [P, WIN, SB * C]) for s in range(2)]
        top = [sb(f"max{i}", [P, PAIRS * HEADS], BF16) for i in range(2)]
        eye16 = sb("eye16", [P, P], BF16)
        probs = [sb(f"probs{i}", [P, 512]) for i in range(3)]
        inv = [sb(f"inv{i}", [P, 2, TOK]) for i in range(2)]
        att_t = [sb(f"att_t{s}", [P, WIN, P]) for s in range(2)]
        z = sb("z", [P, HALVES, HALF])
        hid = sb("hid", [P, HALVES, PAIRS, HALF])
        yt = [sb(f"y{s}", [P, R, UW]) for s in range(2)]

        with ExitStack() as c2:
            sem2 = lambda name: c2.enter_context(nc.semaphore("prep_" + name))
            loaded, scaled, product, copied = (sem2(n) for n in ("loaded", "scaled", "product", "copied"))
            block = c2.enter_context(nc.Block())

            @block.sync
            def _(sp):
                for name, d in w_d.items():
                    sp.dma_start(w[name][tuple(slice(None) for _ in d.shape)], d).then_inc(loaded, 16)

            @block.gpsimd
            def _(pool):
                nc.gpsimd.memset(ones[:, :], 1.0)

            @block.vector
            def _(dve):
                dve.wait_ge(loaded, 16 * len(w_d))
                nc.vector.tensor_copy(eye16[:, :], w["eye"][:, :])
                for t in ks:
                    for p in range(PAIRS):
                        nc.vector.tensor_copy(
                            t[KROWS:, p, :, :].rearrange("k w (h n) -> k w h n", h=HEADS),
                            w["top_rows"][KROWS:KROWS + TOPS, p, :].unsqueeze(1).unsqueeze(3).to_broadcast(
                                [TOPS, WIN, HEADS, TOK]))
                cols = w["cols"]
                for i in range(3):
                    nc.vector.tensor_scalar(scratch[:, i, :], w["qkv"][:, i, :], cols[:, 0:1],
                                            HD ** -0.5 if i == 0 else 1.0, ALU.mult, ALU.mult).then_inc(scaled, 1)
                dve.wait_ge(product, 1)
                nc.vector.tensor_copy(wqkv[:, :, :], misc[0][:, 0:3 * P].rearrange("p (i c) -> p i c", i=3)).then_inc(copied, 1)
                nc.vector.tensor_tensor(bqkv[:, :], misc[1][:, 0:3], cols[:, 4:7], ALU.add).then_inc(copied, 1)
                dve.wait_ge(copied, 2)
                nc.vector.tensor_scalar(bqkv[:, 0:1], bqkv[:, 0:1], HD ** -0.5, None, ALU.mult).then_inc(copied, 1)
                for p in range(PAIRS):
                    nc.vector.tensor_scalar(scratch[:, p, :], w["fc1"][:, p, :], cols[:, 2:3], None, ALU.mult).then_inc(scaled, 1)
                dve.wait_ge(product, 2)
                nc.vector.tensor_copy(w1[:, :, :], misc[0][:, :].rearrange("p (i c) -> p i c", i=PAIRS)).then_inc(copied, 1)
                nc.vector.tensor_tensor(bproj[:, :], misc[1][:, 3:4], cols[:, 7:8], ALU.add).then_inc(copied, 1)
                dve.wait_ge(copied, 5)
                nc.vector.tensor_tensor(by[:, :], bproj[:, :], cols[:, 9:10], ALU.add).then_inc(copied, 1)
                dve.wait_ge(product, 3)
                nc.vector.tensor_tensor(b1[:, :], misc[1][:, 4:5], cols[:, 8:9], ALU.add).then_inc(copied, 1)

            @block.tensor
            def _(pe):
                pe.wait_ge(loaded, 16 * len(w_d))
                cols = w["cols"]
                for i in range(3):
                    nc.tensor.matmul(misc[1][:, i:i + 1], w["qkv"][:, i, :], cols[:, 1:2], start=True, stop=True)
                pe.wait_ge(scaled, 3)
                for i in range(3):
                    last = nc.tensor.matmul(misc[0][:, i * P:(i + 1) * P], w["color1"][:, :], scratch[:, i, :], start=True, stop=True)
                last.then_inc(product, 1)
                pe.wait_ge(copied, 3)
                pe.wait_ge(scaled, 3 + PAIRS)
                for a in range(2):
                    nc.tensor.matmul(misc[1][:, 3:4], w["proj"][:, a, :], bqkv[:, 2:3], start=(a == 0), stop=(a == 1))
                for p in range(PAIRS):
                    last = nc.tensor.matmul(misc[0][:, p * P:(p + 1) * P], w["color2"][:, :], scratch[:, p, :], start=True, stop=True)
                last.then_inc(product, 1)
                pe.wait_ge(copied, 5)
                nc.tensor.matmul(misc[1][:, 4:5], w["fc1"][:, 0, :], cols[:, 3:4], start=True, stop=False)
                nc.tensor.matmul(misc[1][:, 4:5], w1[:, 0, :], bproj[:, 0:1], start=False, stop=True).then_inc(product, 1)

        x_copied, placed_ready = sem("x_copied"), sem("placed_ready")
        x_in = [sem(f"x_in{s}") for s in range(2)]
        qk_parted = sem("qk_parted")
        qk_in = [sem(f"qk_in{s}") for s in range(2)]
        projected, qk_done, v_done, s_done, top_turned, t_done, pv_done = (sem(n) for n in (
            "projected", "qk_done", "v_done", "s_done", "top_turned", "t_done", "pv_done"))
        qk_high, v_ready, max_ready, top_placed, probs_ready, inv_ready, att_t_ready = (sem(n) for n in (
            "qk_high", "v_ready", "max_ready", "top_placed", "probs_ready", "inv_ready", "att_t_ready"))
        z_ready, fc1_done, hid_ready, fc2_done, y_ready = (sem(n) for n in ("z_ready", "fc1_done", "hid_ready", "fc2_done", "y_ready"))
        y_out = [sem(f"y_out{s}") for s in range(2)]
        block = ctx.enter_context(nc.Block())

        QK_MOVES = PARTS * PAIRS * 2
        LAST = UNITS + 1
        has_mlp = lambda u: within(u, 2, UNITS + 2)
        has_att = lambda u: within(u, 1, UNITS + 1)
        has_in = lambda u: within(u, 0, UNITS)

        def unit_at(sup, quarter):
            return lambda t: t[bass.ds(sup * SB + sup // (BPI // SB) + 1, SB)].rearrange(
                "b (c r) w -> (b c) r w", r=R)[:, :, bass.ds(quarter * UW, UW)]

        def run(eng, body, lag=0):
            for u in range(4):
                v = max(u - lag, 0)
                body(u, u % 2, unit_at(v // UPS, v % UPS))
            with eng.Fori(2, UNITS // 2) as k:
                m = k - lag // 2
                for s in range(2):
                    body(k * 2 + s, s, unit_at(m // 2, m % 2 * 2 + s))
            for u in range(UNITS, LAST + 1):
                v = u - lag
                body(u, u % 2, unit_at(v // UPS, v % UPS))

        @block.sync
        def _(sp):
            def move(u, s, window):
                if not has_in(u):
                    return
                if within(u, 2, UNITS):
                    sp.wait_ge(z_ready, HALVES * (u - 1))
                sp.dma_start(xt[s][:, :, :], window(x)).then_inc(x_in[s], 16)
                if within(u, 2, UNITS):
                    sp.wait_ge(t_done, WIN * (u - 1))
                for which, src, dst in ((1, k_headed, ks[s]), (0, q_sided, qs[s])):
                    sp.wait_ge(placed_ready, 8 * u + 8 - 4 * which)
                    for part in range(PARTS):
                        low = int(part == 1 + which)
                        for p in range(PAIRS):
                            stack = dst[part * 2 * C:(part + 1) * 2 * C, p]
                            sp.dma_start(stack.rearrange("k w n -> k (w n)") if which else stack,
                                         src[p * 2 * C:(p + 1) * 2 * C, low, :, :, :].rearrange("p w a n -> p (w a n)"))\
                                .then_inc(qk_in[s], 16)
            run(sp, move)

        @block.gpsimd
        def _(pool):
            def store(u, s, window):
                if has_in(u):
                    pool.wait_ge(x_in[s], (u // 2 + 1) * 16)
                    if within(u, 1, UNITS):
                        pool.wait_ge(v_done, 4 * u)
                    for h in range(HEADS):
                        nc.gpsimd.tensor_tensor(x_twice[:, :, h, :].rearrange("p w (r x) -> p w r x", x=WS),
                                                xt[s][:, :, :].rearrange("p r (w x) -> p w r x", x=WS),
                                                ones[:, :].unsqueeze(2).unsqueeze(3).to_broadcast([P, WIN, R, WS]),
                                                ALU.mult).then_inc(x_copied, 1)
                if has_mlp(u):
                    pool.wait_ge(y_ready, HALVES * (u - 1))
                    pool.dma_start(window(y), yt[s][:, :, :]).then_inc(y_out[s], 16)
            run(pool, store, lag=2)
            for s in range(2):
                pool.wait_ge(y_out[s], 16 * UNITS // 2)

        def columns(t, half):
            return t[:, :, half * HW_:(half + 1) * HW_]

        def by_window(t, half):
            return columns(t, half).rearrange("p r (w x) -> p w r x", x=WS)

        SLICES = WIN + 6
        PROJ, FC1, FC2, QK, V = {1: (0, 1)}, 2, {3: 0, 4: 1}, {5: 0, 6: 1, 7: 2, 8: 3}, {10: 0, 12: 1, 14: 2, 16: 3}
        PLACE = {6: (1, 0), 7: (1, 1), 8: (0, 0), 9: (0, 1)}
        qk_job = lambda q: (q % 2, 1 - q // 2)
        FC1_JOBS = HALVES * PAIRS
        NORMALIZED = WIN // 2
        normalize_at = lambda i: (i - 6) // 2 if i >= 6 and i % 2 == 0 and (i - 6) // 2 < NORMALIZED else None

        @block.tensor
        def _(pe):
            def mlp(u, s, i):
                c = u - 2
                for half in PROJ.get(i, ()):
                    pe.wait_ge(att_t_ready, NORMALIZED * (c + 1))
                    if has_in(u - 1):
                        pe.wait_ge(v_ready, 4 * u - 1 + half)
                    elif c > 0:
                        pe.wait_ge(y_ready, HALVES * c)
                    for a in range(2):
                        last = nc.tensor.matmul(misc[half][:, :], w["proj"][:, a, :],
                                                att_t[s][:, half * WPH:(half + 1) * WPH, a * TOK:(a + 1) * TOK],
                                                start=(a == 0), stop=(a == 1))
                    last.then_inc(projected, 1)
                for j in range(FC1_JOBS if i == FC1 else 0):
                    half, p = divmod(j, PAIRS)
                    if j < 2:
                        pe.wait_ge(z_ready, HALVES * c + j + 1)
                    else:
                        pe.wait_ge(hid_ready, FC1_JOBS * c + j - 1)
                    nc.tensor.matmul(misc[j % 2][:, :], w1[:, p, :], z[:, half, :], start=True, stop=True).then_inc(fc1_done, 1)
                if i in FC2:
                    half = FC2[i]
                    pe.wait_ge(hid_ready, FC1_JOBS * c + FC1_JOBS - 1 + half)
                    for p in range(PAIRS):
                        last = nc.tensor.matmul(misc[half][p * 2 * C:(p + 1) * 2 * C, :], w["fc2"][:, :],
                                                hid[:, half, p, :], start=True, stop=True)
                    last.then_inc(fc2_done, 1)

            def project(u, s, i):
                if i in QK:
                    q = QK[i]
                    half, which = qk_job(q)
                    if q == 0:
                        pe.wait_ge(x_in[s], (u // 2 + 1) * 16)
                    if q > 1:
                        pe.wait_ge(qk_parted, 4 * u + q - 1)
                    elif has_mlp(u):
                        pe.wait_ge(y_ready, HALVES * (u - 2) + q + 1)
                    elif u == 1:
                        pe.wait_ge(v_ready, 3 + q)
                    nc.tensor.matmul(misc[q % 2][:, :], wqkv[:, which, :], by_window(xt[s], half), start=True, stop=True)\
                        .then_inc(qk_done, 1)
                if i in V:
                    v = V[i]
                    if v == 0:
                        pe.wait_ge(x_copied, HEADS * (u + 1))
                    if v < 2:
                        pe.wait_ge(qk_parted, 4 * u + 3 + v)
                    else:
                        pe.wait_ge(v_ready, 4 * u + v - 1)
                    for j in range(4):
                        both = x_twice[:, 4 * v + j, :, :].rearrange("p h n -> p (h n)")
                        last = nc.tensor.matmul(misc[v % 2][:, j * P:(j + 1) * P], both, wqkv[:, 2, :], start=True, stop=True)
                    last.then_inc(v_done, 1)

            def attend(u, s, i):
                b = u - 1
                s = 1 - s
                if i == 0:
                    pe.wait_ge(qk_in[s], (b // 2 + 1) * 16 * QK_MOVES if isinstance(u, int) else
                               (8 * QK_MOVES * (b - s) + 16 * QK_MOVES))
                    pe.wait_ge(v_ready, 4 * b + 4)
                if i < WIN:
                    if within(u, 2, UNITS + 1) or i >= 2:
                        pe.wait_ge(top_placed, WIN * b + i - 1)
                    for p in range(PAIRS):
                        last = nc.tensor.matmul(scores[i % 2][:, p * P:(p + 1) * P], qs[s][0:KROWS, p, i * P:(i + 1) * P],
                                                ks[s][0:KROWS, p, i, :], start=True, stop=True)
                    last.then_inc(s_done, 1)
                if 1 <= i < WIN + 1:
                    j = i - 1
                    pe.wait_ge(max_ready, WIN * b + j + 1)
                    nc.tensor.matmul(scores[j % 2][KROWS:KROWS + TOPS, 0:P], top[j % 2][:, :],
                                     eye16[:, :], start=True, stop=True).then_inc(top_turned, 1)
                if 2 <= i < WIN + 2:
                    j = i - 2
                    pe.wait_ge(top_placed, WIN * b + j + 1)
                    if within(u, 2, UNITS + 1) or j >= 2:
                        pe.wait_ge(probs_ready, WIN * b + j - 1)
                    for p in range(PAIRS):
                        last = nc.tensor.matmul(scores_t[j % 2][:, p * P:(p + 1) * P], ks[s][:, p, j, :],
                                                qs[s][:, p, j * P:(j + 1) * P], start=True, stop=True)
                    last.then_inc(t_done, 1)
                if 4 <= i < WIN + 4:
                    j = i - 4
                    pe.wait_ge(probs_ready, WIN * b + j + 1)
                    if j % 2 == 0 and (within(u, 2, UNITS + 1) or j >= 4):
                        pe.wait_ge(att_t_ready, NORMALIZED * b + j // 2 - 1)
                    tile = weighted[j // 2 % 2]
                    rows = [slice(p * 2 * C, (p + 1) * 2 * C) for p in range(PAIRS)]
                    for p in range(PAIRS):
                        nc.tensor.matmul(tile[rows[p], j % 2 * P:(j % 2 + 1) * P], vt[s][:, j, rows[p]],
                                         probs[j % 3][:, p * P:(p + 1) * P], start=True, stop=True)
                    for a in range(2):
                        for p in range(PAIRS):
                            last = nc.tensor.matmul(tile[rows[p], 2 * P + j % 2 * TOK:2 * P + (j % 2 + 1) * TOK],
                                                    w["head_mask"][:, a, :],
                                                    probs[j % 3][:, (2 * p + a) * TOK:(2 * p + a + 1) * TOK],
                                                    start=(a == 0), stop=(a == 1))
                    last.then_inc(pv_done, 1)

            def step(u, s, _):
                for i in range(SLICES):
                    if has_att(u):
                        attend(u, s, i)
                    if has_mlp(u):
                        mlp(u, s, i)
                    if has_in(u):
                        project(u, s, i)
            run(pe, step)

        @block.scalar
        def _(act):
            def attend(u, s, i):
                b = u - 1
                if 1 <= i < WIN + 1:
                    j = i - 1
                    act.wait_ge(top_turned, WIN * b + j + 1)
                    nc.scalar.activation(qs[1 - s][KROWS:, :, j * P:(j + 1) * P],
                                         scores[j % 2][KROWS:KROWS + TOPS, 0:P].unsqueeze(1).to_broadcast([TOPS, PAIRS, P]),
                                         ACT.Copy, scale=1 / TOP_SCALE).then_inc(top_placed, 1)
                if 2 <= i < WIN + 2:
                    j = i - 2
                    act.wait_ge(t_done, WIN * b + j + 1)
                    if within(u, 2, UNITS + 1) or j >= 3:
                        act.wait_ge(pv_done, WIN * b + j - 2)
                    nc.scalar.activation(probs[j % 3][:, :], scores_t[j % 2][:, :], ACT.Exp).then_inc(probs_ready, 1)

            def step(u, s, _):
                for i in range(SLICES):
                    if has_att(u):
                        attend(u, s, i)
                    for j in range(FC1_JOBS if i == FC1 and has_mlp(u) else 0):
                        act.wait_ge(fc1_done, FC1_JOBS * (u - 2) + j + 1)
                        if within(u, 3, UNITS + 2) and j % PAIRS == 0:
                            act.wait_ge(fc2_done, HALVES * (u - 3) + j // PAIRS + 1)
                        nc.scalar.activation(hid[:, j // PAIRS, j % PAIRS, :], misc[j % 2][:, :], ACT.Gelu,
                                             bias=b1[:, 0:1]).then_inc(hid_ready, 1)
                    if i in QK and has_in(u):
                        half, which = qk_job(QK[i])
                        act.wait_ge(qk_done, 4 * u + QK[i] + 1)
                        if QK[i] == 0 and within(u, 1, UNITS):
                            act.wait_ge(placed_ready, 8 * u)
                        nc.scalar.activation(qk_split[:, 2 * which, half * HALF:(half + 1) * HALF], misc[QK[i] % 2][:, :],
                                             ACT.Identity, bias=bqkv[:, which:which + 1]).then_inc(qk_high, 1)
            run(act, step)

        @block.vector
        def _(dve):
            def mlp(u, s, i):
                c = u - 2
                for half in PROJ.get(i, ()):
                    dve.wait_ge(projected, HALVES * c + half + 1)
                    if within(u, 3, UNITS + 2) and half == 0:
                        dve.wait_ge(y_ready, HALVES * c)
                    nc.vector.tensor_tensor(
                        z[:, half, :].rearrange("p (r w x) -> p r w x", r=R, x=WS),
                        misc[half][:, :].rearrange("p (w r x) -> p r w x", r=R, x=WS),
                        columns(xt[s], half).rearrange("p r (w x) -> p r w x", x=WS), ALU.add).then_inc(z_ready, 1)
                if i in FC2:
                    half = FC2[i]
                    if half == 0 and within(u, 4, UNITS + 2):
                        dve.wait_ge(y_out[s], (8 * (u - s) - 16) if not isinstance(u, int) else 16 * (u // 2 - 1))
                    dve.wait_ge(fc2_done, HALVES * c + half + 1)
                    nc.vector.scalar_tensor_tensor(
                        columns(yt[s], half), misc[half][:, :].rearrange("p (r x) -> p r x", r=R), by[:, 0:1],
                        z[:, half, :].rearrange("p (r x) -> p r x", r=R), ALU.add, ALU.add).then_inc(y_ready, 1)

            def project(u, s, i):
                if i in QK:
                    half, which = qk_job(QK[i])
                    high = qk_split[:, 2 * which, half * HALF:(half + 1) * HALF]
                    low = qk_split[:, 2 * which + 1, half * HALF:(half + 1) * HALF]
                    dve.wait_ge(qk_high, 4 * u + QK[i] + 1)
                    nc.vector.scalar_tensor_tensor(low, misc[QK[i] % 2][:, :], bqkv[:, which:which + 1], high,
                                                   ALU.add, ALU.subtract).then_inc(qk_parted, 1)
                if i in PLACE:
                    which, part = PLACE[i]
                    dst, marks = ((q_sided, w["sides"]), (k_headed, w["key_heads"]))[which]
                    dve.wait_ge(qk_parted, 4 * u + 4 - 2 * which)
                    if part == 0 and within(u, 2, UNITS):
                        dve.wait_ge(qk_in[1 - s], 8 * QK_MOVES * (u - s) + s * 16 * QK_MOVES if not isinstance(u, int)
                                    else 16 * QK_MOVES * ((u + 1) // 2))
                    elif part == 0 and u == 1:
                        dve.wait_ge(qk_in[0], 16 * QK_MOVES)
                    for copy in range(2):
                        nc.vector.tensor_scalar(dst[:, part, :, copy, :],
                                                qk_split[:, 2 * which + part, :].rearrange("p (w n) -> p w n", n=TOK),
                                                marks[:, copy:copy + 1], None, ALU.mult).then_inc(placed_ready, 1)
                if i in V:
                    dve.wait_ge(v_done, 4 * u + V[i] + 1)
                    if V[i] == 0 and within(u, 2, UNITS):
                        dve.wait_ge(pv_done, WIN * (u - 1))
                    nc.vector.tensor_tensor(vt[s][:, 4 * V[i]:4 * V[i] + 4, :].rearrange("p w (g c) -> p (w g) c", c=C),
                                            misc[V[i] % 2][:, :].rearrange("p (w c) -> p w c", c=C),
                                            w["head_mask"][:, 0, 0:C].unsqueeze(1).to_broadcast([P, 4 * SB, C]),
                                            ALU.mult).then_inc(v_ready, 1)

            def attend(u, s, i):
                b = u - 1
                if i < WIN:
                    dve.wait_ge(s_done, WIN * b + i + 1)
                    if within(u, 2, UNITS + 1) or i >= 2:
                        dve.wait_ge(top_turned, WIN * b + i - 1)
                    nc.vector.tensor_reduce(top[i % 2][:, :], scores[i % 2][:, :].rearrange("p (k m) -> p k m", m=TOK),
                                            AX.X, ALU.max).then_inc(max_ready, 1)
                j = normalize_at(i)
                if j is not None:
                    dve.wait_ge(pv_done, WIN * b + 2 * j + 2)
                    sums = weighted[j % 2][:, 2 * P:2 * P + 2 * TOK].rearrange("p (w n) -> p w n", w=2)
                    nc.vector.reciprocal(inv[j % 2][:, :, :], sums).then_inc(inv_ready, 1)
                    dve.wait_ge(inv_ready, NORMALIZED * b + j + 1)
                    if j == 0 and within(u, 3, UNITS + 1):
                        dve.wait_ge(projected, HALVES * (u - 2))
                    nc.vector.tensor_tensor(att_t[1 - s][:, 2 * j:2 * j + 2, :].rearrange("p w (a n) -> p w a n", a=2),
                                            weighted[j % 2][:, 0:2 * P].rearrange("p (w a n) -> p w a n", w=2, a=2),
                                            inv[j % 2][:, :, :].unsqueeze(2).to_broadcast([P, 2, 2, TOK]),
                                            ALU.mult).then_inc(att_t_ready, 1)

            def step(u, s, _):
                for i in range(SLICES):
                    if has_att(u):
                        attend(u, s, i)
                    if has_mlp(u):
                        mlp(u, s, i)
                    if has_in(u):
                        project(u, s, i)
            run(dve, step)


def program(nc, x, pos_taps, eye, pos_b, taps, conv_b, color1, qkv, proj, color2, fc1, fc2, cols, head_mask, sides,
            key_heads, top_rows, out):
    dram = lambda name, shape, dt=F32: nc.dram_tensor(name, shape, dt, kind="Internal").ap()
    y = [dram(f"y{i}", [PB, P, W]) for i in range(4)]
    edges_x = dram("edges_x", [2, PB, C, W])
    h_edges = [dram(f"edges_h{i}", [2, PB, 2, C, W], F16) for i in range(3)]
    zero_borders(nc, y, [edges_x], h_edges)
    position_conv(nc, x, pos_taps, eye, pos_b, edges_x, y[0])
    attention_mlp(nc, dict(color1=color1, qkv=qkv, proj=proj, color2=color2, fc1=fc1, fc2=fc2, cols=cols,
                           head_mask=head_mask, sides=sides, key_heads=key_heads, top_rows=top_rows, eye=eye),
                  y[0], y[1])
    for i in range(3):
        residual_pair(nc, f"layer{i + 1}", taps[2 * i], taps[2 * i + 1], conv_b[2 * i], conv_b[2 * i + 1],
                      y[i + 1], i == 0, out if i == 2 else y[i + 2], i == 2, h_edges[i])


_ORDER = ["x", "pos_taps", "eye", "pos_b", "taps", "conv_b", "color1", "qkv", "proj", "color2", "fc1", "fc2", "cols",
          "head_mask", "sides", "key_heads", "top_rows"]


def kernel(**inputs):
    import numpy as np
    import concourse.bacc as _bacc
    from concourse import mybir as _mybir
    from concourse.bass_utils import run_bass_kernel_spmd as _run

    def banded(w):
        t = np.zeros((P, TAPS + 1, P), np.float32)
        for r in range(R):
            cols = slice(r * C, (r + 1) * C)
            for ky in range(3):
                for kx in range(3):
                    r_in, m = r + ky - 1, w[:, :, ky, kx].T
                    if 0 <= r_in < R:
                        t[r_in * C:(r_in + 1) * C, kx, cols] = m
                    else:
                        p0 = (kx * 2 + (r_in == R)) * C
                        t[p0:p0 + C, TAPS, cols] = m
        return t

    a = {k: np.asarray(v) for k, v in inputs.items()}
    depthwise = np.zeros((C, C, 3, 3), np.float32)
    depthwise[np.arange(C), np.arange(C)] = a["L0_conv_pos_w"][:, 0]
    arrays = {"x": np.ascontiguousarray(a["x"]), "pos_taps": banded(depthwise), "eye": np.eye(P, dtype=np.float32),
              "pos_b": np.tile(a["L0_conv_pos_b"], R).reshape(P, 1),
              "taps": np.stack([banded(a[f"L{i}_conv_w{j}"]) for i in (1, 2, 3) for j in (1, 2)]),
              "conv_b": np.stack([np.tile(a[f"L{i}_conv_b{j}"], R).reshape(P, 1) for i in (1, 2, 3) for j in (1, 2)])}

    def diagonal(m, blocks=range(SB)):
        t = np.zeros((P, P), np.float32)
        for g in blocks:
            t[g * C:(g + 1) * C, g * C:(g + 1) * C] = m
        return t

    fc1, fc2 = np.zeros((P, PAIRS, P), np.float32), np.zeros((P, 2 * C), np.float32)
    for side in range(2):
        fc2[side * HID:(side + 1) * HID, side * C:(side + 1) * C] = a["L0_conv_fc2_w"].T
    for p in range(PAIRS):
        for side in range(2):
            g = 2 * p + side
            fc1[g * C:(g + 1) * C, p, side * HID:(side + 1) * HID] = a["L0_conv_fc1_w"].T
    qkv_w, qkv_b = a["L0_conv_qkv_w"], a["L0_conv_qkv_b"]
    column = lambda v: np.tile(v.reshape(-1), P // v.size)
    mask = np.zeros((P, 2, 2 * C), np.float32)
    for side in range(2):
        for h in range(HEADS):
            mask[h * TOK:(h + 1) * TOK, side, side * C + h * HD:side * C + (h + 1) * HD] = 1.0
    top_rows = np.zeros((P, PAIRS, HEADS), np.float32)
    top_rows[KROWS + np.arange(PAIRS * HEADS)] = -TOP_SCALE * np.eye(PAIRS * HEADS).reshape(-1, PAIRS, HEADS)
    arrays.update(
        color1=diagonal(a["L0_conv_color1"]), color2=diagonal(a["L0_conv_color2"]),
        qkv=np.stack([diagonal(qkv_w[i * C:(i + 1) * C].T) for i in range(3)], axis=1),
        proj=np.stack([diagonal(a["L0_conv_proj_w"].T, range(side, SB, 2)) for side in range(2)], axis=1),
        fc1=fc1, fc2=fc2, head_mask=mask,
        sides=np.repeat(np.tile(np.eye(2, dtype=np.float32), (PAIRS, 1)), C, axis=0),
        key_heads=np.repeat(np.tile(np.eye(HEADS, dtype=np.float32), (SB, 1)), HD, axis=0), top_rows=top_rows,
        cols=np.stack([column(v) for v in (
            a["L0_conv_alpha1"], a["L0_conv_beta1"], a["L0_conv_alpha2"], a["L0_conv_beta2"],
            qkv_b[0:C], qkv_b[C:2 * C], qkv_b[2 * C:], a["L0_conv_proj_b"], a["L0_conv_fc1_b"], a["L0_conv_fc2_b"])], axis=1))
    nc = _bacc.Bacc("TRN2", target_bir_lowering=False, num_devices=1)
    args = [nc.dram_tensor("in_" + k, arrays[k].shape, _mybir.dt.from_np(arrays[k].dtype), kind="ExternalInput").ap()
            for k in _ORDER]
    args.append(nc.dram_tensor("out", (IMAGES, C, H, W), F32, kind="ExternalOutput").ap())
    program(nc, *args)
    r = _run(nc, [{"in_" + k: v for k, v in arrays.items()}], core_ids=[0])
    return r.results[0]["out"]
```
